# Optimizing a Trainium2 kernel written in Bass

```python
import numpy as np
import jax
import jax.numpy as jnp

def _softmax(x, axis=-1):
    return jax.nn.softmax(x, axis=axis)

def _gelu(x):
    return jax.nn.gelu(x, approximate=True)

def _silu(x):
    return jax.nn.silu(x)

def _sigmoid(x):
    return jax.nn.sigmoid(x)

def _layernorm(x, axis=-1, eps=1e-05):
    m = jnp.mean(x, axis=axis, keepdims=True)
    v = jnp.var(x, axis=axis, keepdims=True)
    return (x - m) / jnp.sqrt(v + eps)

def _scatter_add(tgt, idx, src, axis=0):
    return tgt.at[idx].add(src)

def _segment_sum(src, seg, n):
    return jax.ops.segment_sum(src, seg, n)
kernel_name = 'mk_xattn_ffn_d1_seqx_r8_bf5086'

def setup_inputs(seed: int=0):
    np.random.seed(seed)
    _w = jnp.asarray

    def _rec_inputs():
        import jax
        import jax.numpy as jnp
        _rk = jax.random.key(seed)
        x = 7.22e-05 + 1 * jax.random.normal(jax.random.fold_in(_rk, 1), (16, 256, 128), jnp.float32)
        _lenS = 256 - jax.random.randint(jax.random.fold_in(_rk, 7), (16,), 0, max(1, 256 // 4) + 1, jnp.int32)
        _lenS2 = 64 - jax.random.randint(jax.random.fold_in(_rk, 8), (16,), 0, max(1, 64 // 4) + 1, jnp.int32)
        _ctx_1024P = jax.random.normal(jax.random.fold_in(_rk, 11), (16, 16, 128), jnp.float32)
        _ctx_1024c = jax.random.dirichlet(jax.random.fold_in(_rk, 511), 0.3 * jnp.ones((16,), jnp.float32), (16, 64))
        _ctx_1024t = jnp.einsum('bsk,bkd->bsd', _ctx_1024c, _ctx_1024P)
        _ctx_1024t = _ctx_1024t * jax.lax.rsqrt(jnp.mean(jnp.square(_ctx_1024t)) + 1e-12) * 0.953939
        ctx_1024 = 4.13588e-05 + 0.999923 * (_ctx_1024t + 0.3 * jax.random.normal(jax.random.fold_in(_rk, 611), (16, 64, 128), jnp.float32))
        return (x, ctx_1024)
    x, ctx_1024 = _rec_inputs()

    def _L0_xattn_setup():
        import jax, jax.numpy as jnp
        import numpy as np
        D_MODEL = 128
        N_HEADS = 16
        D_K = D_MODEL // N_HEADS
        B, S = (4, 256)
        key = jax.random.key(seed)
        ks = jax.random.split(key, 11)
        scale = 1.0 / np.sqrt(D_MODEL)
        inp = {'query': jax.random.normal(ks[0], (B, S, D_MODEL), jnp.float32), 'key_': jax.random.normal(ks[1], (B, S, D_MODEL), jnp.float32), 'value': jax.random.normal(ks[2], (B, S, D_MODEL), jnp.float32), 'W_Q': jax.random.normal(ks[3], (D_MODEL, D_MODEL), jnp.float32) * scale, 'b_Q': jnp.zeros((D_MODEL,), jnp.float32), 'W_K': jax.random.normal(ks[4], (D_MODEL, D_MODEL), jnp.float32) * scale, 'b_K': jnp.zeros((D_MODEL,), jnp.float32), 'W_V': jax.random.normal(ks[5], (D_MODEL, D_MODEL), jnp.float32) * scale, 'b_V': jnp.zeros((D_MODEL,), jnp.float32), 'W_O': jax.random.normal(ks[6], (D_MODEL, D_MODEL), jnp.float32) * scale, 'b_O': jnp.zeros((D_MODEL,), jnp.float32)}
        return inp
    _L0_xattn_all = _L0_xattn_setup()
    _L0_xattn_in = {k: v for k, v in _L0_xattn_all.items() if k in ('W_Q', 'b_Q', 'W_K', 'b_K', 'W_V', 'b_V', 'W_O', 'b_O')}
    del _L0_xattn_all

    def _L0_ffn_setup():
        import jax, jax.numpy as jnp
        import numpy as np
        EPS = 1e-05
        HEADS = 8
        DIM_KEY = 128
        K = 16
        NUM_KEYS = 32
        key = jax.random.key(seed)
        ks = jax.random.split(key, 5)
        B, T, D = (1, 128, 128)
        x = jax.random.normal(ks[0], (B, T, D), dtype=jnp.float32)
        norm_w = jnp.ones((D,), dtype=jnp.float32)
        wq = jax.random.normal(ks[1], (D, DIM_KEY * HEADS * 2), dtype=jnp.float32) * 0.02
        keys = jax.random.normal(ks[2], (HEADS, NUM_KEYS, 2, DIM_KEY), dtype=jnp.float32) * 0.02
        expert_down = jax.random.normal(ks[3], (NUM_KEYS * NUM_KEYS, D), dtype=jnp.float32) * 0.02
        expert_up = jax.random.normal(ks[4], (NUM_KEYS * NUM_KEYS, D), dtype=jnp.float32) * 0.02
        return {'x': x, 'norm_w': norm_w, 'wq': wq, 'keys': keys, 'expert_down': expert_down, 'expert_up': expert_up}
    _L0_ffn_all = _L0_ffn_setup()
    _L0_ffn_in = {k: v for k, v in _L0_ffn_all.items() if k in ('norm_w', 'wq', 'keys', 'expert_down', 'expert_up')}
    del _L0_ffn_all
    return {'x': x, 'ctx_1024': ctx_1024, 'L0_xattn_W_Q': _L0_xattn_in['W_Q'], 'L0_xattn_b_Q': _L0_xattn_in['b_Q'], 'L0_xattn_W_K': _L0_xattn_in['W_K'], 'L0_xattn_b_K': _L0_xattn_in['b_K'], 'L0_xattn_W_V': _L0_xattn_in['W_V'], 'L0_xattn_b_V': _L0_xattn_in['b_V'], 'L0_xattn_W_O': _L0_xattn_in['W_O'], 'L0_xattn_b_O': _L0_xattn_in['b_O'], 'L0_ffn_norm_w': _L0_ffn_in['norm_w'], 'L0_ffn_wq': _L0_ffn_in['wq'], 'L0_ffn_keys': _L0_ffn_in['keys'], 'L0_ffn_expert_down': _L0_ffn_in['expert_down'], 'L0_ffn_expert_up': _L0_ffn_in['expert_up']}

def reference(x, ctx_1024, L0_xattn_W_Q, L0_xattn_b_Q, L0_xattn_W_K, L0_xattn_b_K, L0_xattn_W_V, L0_xattn_b_V, L0_xattn_W_O, L0_xattn_b_O, L0_ffn_norm_w, L0_ffn_wq, L0_ffn_keys, L0_ffn_expert_down, L0_ffn_expert_up):
    import jax
    import jax.numpy as jnp

    def _L0_xattn_ref(query, key_, value, W_Q, b_Q, W_K, b_K, W_V, b_V, W_O, b_O):
        import jax, jax.numpy as jnp
        import numpy as np
        D_MODEL = 128
        N_HEADS = 16
        D_K = D_MODEL // N_HEADS
        B, S = (4, 256)
        b = query.shape[0]

        def split_heads(x):
            return x.reshape(b, -1, N_HEADS, D_K).transpose(0, 2, 1, 3)
        Q = split_heads(query @ W_Q.T + b_Q)
        K = split_heads(key_ @ W_K.T + b_K)
        V = split_heads(value @ W_V.T + b_V)
        scores = jnp.einsum('bhqd,bhkd->bhqk', Q, K) / jnp.sqrt(jnp.float32(D_K))
        weights = jax.nn.softmax(scores, axis=-1)
        attn = jnp.einsum('bhqk,bhkd->bhqd', weights, V)
        attn = attn.transpose(0, 2, 1, 3).reshape(b, -1, D_MODEL)
        out = attn @ W_O.T + b_O
        return out

    def _L0_ffn_ref(x, norm_w, wq, keys, expert_down, expert_up):
        import jax, jax.numpy as jnp
        import numpy as np
        EPS = 1e-05
        HEADS = 8
        DIM_KEY = 128
        K = 16
        NUM_KEYS = 32
        B, T, D = x.shape
        inv = jax.lax.rsqrt(jnp.mean(x * x, axis=-1, keepdims=True) + EPS)
        x_norm = x * inv * norm_w
        q = (x_norm @ wq).reshape(B, T, HEADS, 2, DIM_KEY)
        sim = jnp.einsum('bthpd,hkpd->pbthk', q, keys)
        s1, i1 = jax.lax.top_k(sim[0], K)
        s2, i2 = jax.lax.top_k(sim[1], K)
        all_idx = (i1[..., :, None] * NUM_KEYS + i2[..., None, :]).reshape(B, T, HEADS, K * K)
        all_scores = (s1[..., :, None] + s2[..., None, :]).reshape(B, T, HEADS, K * K)
        final_scores, pk = jax.lax.top_k(all_scores, K)
        final_idx = jnp.take_along_axis(all_idx, pk, axis=-1)
        wd = expert_down[final_idx]
        wu = expert_up[final_idx]
        hidden = jnp.einsum('btd,bthkd->bthk', x_norm, wd)
        hidden = jax.nn.gelu(hidden, approximate=False)
        hidden = hidden * jax.nn.relu(final_scores)
        out = jnp.einsum('bthk,bthkd->btd', hidden, wu)
        return out
    x = x + _L0_xattn_ref(_layernorm(x, axis=-1), ctx_1024, ctx_1024, L0_xattn_W_Q, L0_xattn_b_Q, L0_xattn_W_K, L0_xattn_b_K, L0_xattn_W_V, L0_xattn_b_V, L0_xattn_W_O, L0_xattn_b_O)
    x = x + _L0_ffn_ref(_layernorm(x, axis=-1), L0_ffn_norm_w, L0_ffn_wq, L0_ffn_keys, L0_ffn_expert_down, L0_ffn_expert_up)
    return x

_drawn_inputs = setup_inputs


def setup_inputs(seed=0):
    import zlib

    import numpy as np

    out = dict(_drawn_inputs(seed))
    spreads = {'L0_xattn_b_Q': (0.0, 0.41),
     'L0_xattn_b_K': (0.0, 0.8),
     'L0_xattn_b_V': (0.0, 0.1),
     'L0_xattn_b_O': (0.0, 0.1),
     'L0_ffn_norm_w': (1.0, 0.6)}
    factors = {'L0_ffn_wq': 8.0, 'L0_ffn_keys': 8.0, 'L0_ffn_expert_down': 8.0, 'L0_ffn_expert_up': 8.0}
    for name, (base, spread) in spreads.items():
        noise = np.random.default_rng([zlib.crc32(name.encode()), seed]).standard_normal(out[name].shape)
        drawn = base * np.exp(spread * noise) if base else spread * noise
        out[name] = jnp.asarray(drawn.astype(out[name].dtype))
    for name, factor in factors.items():
        out[name] = (out[name] * factor).astype(out[name].dtype)
    return out
```

```python
from contextlib import ExitStack

import concourse.bass as bass
from concourse import mybir

ALU = mybir.AluOpType
ACT = mybir.ActivationFunctionType
AX = mybir.AxisListType
F32 = mybir.dt.float32
F32R = mybir.dt.float32r
BF16 = mybir.dt.bfloat16

P = 128
D = 128
BATCH, SEQ, CTX = 16, 256, 64
TILES = SEQ // P
HEADS, DK = 16, 8
PAIRS = HEADS // 2
EPS = 1e-5
RH, NK, TOP = 8, 32, 16
EXPERTS = NK * NK
CHUNKS = EXPERTS // P
HALF = 512
LOWEST = -3.0e38
TINY = 1e-37
STEEP = float(2 ** 30)
MARGIN = float(2 ** -20)

RECTS = [(0, 1, 16), (1, 1, 8), (2, 2, 5), (4, 4, 3), (8, 8, 1)]
CANDS = sum(n * m for _, n, m in RECTS)

ACT_HEADS = (1, 4, 6)
DVE_SLOTS, ACT_SLOTS = 3, 2


def on_act(h):
    return h in ACT_HEADS


def heads_before(tile, h, act):
    kind = [on_act(x) == act for x in range(RH)]
    return tile * sum(kind) + sum(kind[:h])


def misc_plan(attend, route):
    order = []
    if route:
        order += [(f"hidden{c}", "act") for c in range(4)]
    if attend:
        order += [("ctxT", "act"), ("yT", "act"), ("qkv", "act")]
        order += [(f"scores{t}{s}", "act") for t in range(TILES) for s in range(2)]
    if route:
        order += [("simsT00", "act"), ("simsT01", "act")]
    if attend:
        order += [("probsT00", "act"), ("probsT01", "act"), ("attn0", "dve"),
                  ("probsT10", "act"), ("probsT11", "act"), ("attn1", "dve"),
                  ("attnT0", "act"), ("attnT1", "act"), ("proj", "dve")]
    if route:
        order += [("simsT10", "act"), ("simsT11", "act"), ("out0", "dve")]
    if attend:
        order += [("normT", "act"), ("sims0", "act"), ("sims1", "act")]
    if route:
        order += [("out1", "dve")]
    plan, used, read = {}, [0, 0], {}
    for n, (name, reader) in enumerate(order):
        b = n % 2
        k = read.get((b, reader), 0)
        plan[name] = (b, used[b], k, reader)
        used[b] += 1
        read[(b, reader)] = k + 1
    return plan, used, read


def xattn_peer_kernel(nc, x, ctx, W_Q, b_Q, W_K, b_K, W_V, b_V, W_O, b_O,
                      norm_w, wq, keys, down, up, eye, spread, head_mask, key_mask, out):
    with ExitStack() as stack:
        def sb(name, shape, dt=F32):
            return stack.enter_context(nc.sbuf_tensor(name, shape, dt))

        def sem(name):
            return stack.enter_context(nc.semaphore(name))

        ident = sb("ident", [P, P])
        neg_ident = sb("neg_ident", [P, P], BF16)
        spread_f = sb("spread_f", [P, EXPERTS])
        spread_r = sb("spread_r", [P, EXPERTS], F32R)
        mask = sb("mask", [P, HEADS])
        pair_mask = sb("pair_mask", [P, 2])
        pool_mark = sb("pool_mark", [P, 1])
        v_biased = sb("v_biased", [P, D])
        w_nat = sb("w_nat", [P, 4, D])
        wT = sb("wT", [P, 4, D])
        bq = sb("bq", [P, 1])
        bk = sb("bk", [P, 1])
        bk_scaled = sb("bk_scaled", [P, 1])
        bv = sb("bv", [P, D])
        bo = sb("bo", [P, D])
        nw = sb("nw", [P, 1])
        wq_nat = sb("wq_nat", [P, 2 * RH, P])
        wqT = sb("wqT", [P, 2 * RH, P])
        keys_nat = sb("keys_nat", [P, 2, 2, P])
        keysT = sb("keysT", [P, 2, 2, P])
        sim_w = sb("sim_w", [P, RH * 2 * NK])
        down_nat = sb("down_nat", [P, CHUNKS, D])
        downT = sb("downT", [P, CHUNKS, P])
        up_sb = sb("up_sb", [P, CHUNKS, D])
        neg_half = sb("neg_half", [P, TILES])

        x_in = sb("x_in", [P, TILES, D])
        ctx_in = sb("ctx_in", [P, D])
        x_bias = sb("x_bias", [P, TILES, D])
        stats = sb("stats", [P, TILES, 6])
        mean_var = sb("mean_var", [P, TILES, 2])
        stats2 = sb("stats2", [P, TILES, 6])
        mean_var2 = sb("mean_var2", [P, TILES, 2])
        shifted_var = sb("shifted_var", [P, TILES])
        rstd = sb("rstd", [P, TILES])
        shifted_var2 = sb("shifted_var2", [P, TILES])
        rstd2 = sb("rstd2", [P, TILES])
        y = sb("y", [P, TILES, D])
        yT = sb("yT", [P, SEQ])
        ctxT = sb("ctxT", [P, P])
        qT = sb("qT", [P, SEQ])
        kT = sb("kT", [P, CTX])
        v_in = sb("v_in", [P, D])
        k_blocks = sb("k_blocks", [P, HEADS, CTX])
        v_blocks = sb("v_blocks", [P, PAIRS, 2, DK + 1])
        scores = sb("scores", [P, TILES, HEADS, CTX])
        peak = sb("peak", [P, TILES, HEADS])
        probsT = sb("probsT", [P, TILES, PAIRS, P])
        rsum = sb("rsum", [P, TILES, HEADS])
        attn = sb("attn", [P, TILES, D])
        attnT = sb("attnT", [P, TILES, P])
        x1_new = sb("x1_new", [P, TILES, D])
        x1 = sb("x1", [P, TILES, D])
        xn = sb("xn", [P, TILES, D])
        xnT = sb("xnT", [P, SEQ])
        flag = sb("flag", [P, 8])

        sims = sb("sims", [P, TILES, RH, 2, NK])
        sims_hl = sb("sims_hl", [P, TILES, RH, 2, 2 * NK], F32R)
        simsT = sb("simsT", [P, TILES, RH, P], F32R)
        sorted16 = sb("sorted16", [P, TILES, RH, 2, TOP])
        rest = sb("rest", [P, TILES, RH, 2, NK])
        cands = sb("cands", [P, TILES, RH, CANDS])
        cands_rest = sb("cands_rest", [P, TILES, RH, CANDS])
        best = sb("best", [P, TILES, RH, TOP])
        top_sim = sb("top_sim", [P, TILES, RH])
        cut_raw = sb("cut_raw", [P, TILES, RH])
        cut = sb("cut", [P, TILES, RH])
        steep_cut = sb("steep_cut", [P, TILES, RH])
        kept_d = sb("kept_d", [P, DVE_SLOTS, 2, HALF])
        kept_a = sb("kept_a", [P, ACT_SLOTS, 2, HALF])
        pair_sums = sb("pair_sums", [P, 2, 2, HALF])
        below = sb("below", [P, 2, 2, HALF], BF16)
        geluT = sb("geluT", [P, CHUNKS, SEQ])
        gatedT = sb("gatedT", [P, CHUNKS, P])
        y_out = sb("y_out", [P, TILES, D])
        mark = sb("mark", [P, 8])

        pair_ps = [stack.enter_context(nc.psum_tensor(f"pair_ps{n}", [P, HALF], F32)) for n in range(4)]
        score_ps = [stack.enter_context(nc.psum_tensor(f"score_ps{n}", [P, HALF], F32)) for n in range(2)]
        misc_ps = [stack.enter_context(nc.psum_tensor(f"misc_ps{n}", [P, HALF], F32)) for n in range(2)]
        banks = pair_ps + score_ps + misc_ps

        loaded = sem("loaded")
        setup_dve = sem("setup_dve")
        setup_pe = sem("setup_pe")
        setup_act = sem("setup_act")
        setup_pool = sem("setup_pool")
        x_loaded = sem("x_loaded")
        ctx_loaded = sem("ctx_loaded")
        inputs_read = sem("inputs_read")
        var_ready = sem("var_ready")
        rstd_ready = sem("rstd_ready")
        y_ready = sem("y_ready")
        v_ready = sem("v_ready")
        k_blocks_ready = sem("k_blocks_ready")
        v_blocks_ready = sem("v_blocks_ready")
        scores_ready = sem("scores_ready")
        peak_ready = sem("peak_ready")
        shifted = sem("shifted")
        xn_ready = sem("xn_ready")
        sims_for_topk = sem("sims_for_topk")
        sims_to_split = sem("sims_to_split")
        sims_split = sem("sims_split")
        halves_sorted = sem("halves_sorted")
        cands_ready = sem("cands_ready")
        cut_ready = sem("cut_ready")
        pairs_ready = sem("pairs_ready")
        pairs_copied = sem("pairs_copied")
        below_ready = sem("below_ready")
        lowered = sem("lowered")
        kept_by_dve = sem("kept_by_dve")
        kept_by_act = sem("kept_by_act")
        kept_d_read = sem("kept_d_read")
        kept_a_read = sem("kept_a_read")
        score_ready = sem("score_ready")
        gelu_ready = sem("gelu_ready")
        gated = sem("gated")
        out_ready = sem("out_ready")
        out_stored = sem("out_stored")
        out_stored_dve = sem("out_free")
        misc_for = {(b, e): sem(f"misc{b}_for_{e}") for b in range(2) for e in ("act", "dve")}
        misc_read = [sem(f"misc{b}_read") for b in range(2)]
        dve_step = sem("dve_step")
        pool_step = sem("pool_step")

        x_v = x.rearrange("b (t p) d -> b p t d", p=P)
        out_v = out.rearrange("b (t p) d -> b p t d", p=P)

        block = stack.enter_context(nc.Block())

        @block.sync
        def _(sp):
            loads = [
                (ident[:], eye), (w_nat[:, 0, :], W_Q), (w_nat[:, 1, :], W_K), (w_nat[:, 2, :], W_V),
                (w_nat[:, 3, :], W_O), (nw[:], norm_w.rearrange("(p o) -> p o", o=1)),
                (bq[:], b_Q.rearrange("(p o) -> p o", o=1)), (bk[:], b_K.rearrange("(p o) -> p o", o=1)),
                (wq_nat[:].rearrange("p c d -> p (c d)"), wq),
            ]
            loads += [(keys_nat[:, g, :, :], keys[4 * g:4 * g + 4].rearrange("h k s d -> (h k) s d")) for g in range(2)]
            loads += [
                (down_nat[:], down.rearrange("(c p) d -> p c d", p=P)),
                (up_sb[:], up.rearrange("(c p) d -> p c d", p=P)),
                (spread_f[:], spread), (mask[:], head_mask), (pair_mask[:], key_mask),
                (bv[:], b_V.rearrange("(o d) -> o d", o=1).to_broadcast([P, D])),
                (bo[:], b_O.rearrange("(o d) -> o d", o=1).to_broadcast([P, D])),
            ]
            for dst, src in loads:
                sp.dma_start(dst, src).then_inc(loaded, 16)
            assert len(loads) == 18

            def load_batch(b):
                sp.dma_start(x_in[:], x_v[b]).then_inc(x_loaded, 16)
                sp.dma_start(ctx_in[0:CTX, :], ctx[b]).then_inc(ctx_loaded, 16)
                sp.dma_start(ctx_in[CTX:P, :], ctx[b]).then_inc(ctx_loaded, 16)

            def store_batch(b):
                for t in range(TILES):
                    sp.wait_ge(out_ready, t + 1)
                    sp.dma_start(out_v[b, :, t, :], y_out[:, t, :]).then_inc(out_stored, 16)
                sp.sem_inc(out_ready, -TILES)
                sp.wait_ge(out_stored, 16 * TILES)
                sp.sem_inc(out_stored, -16 * TILES)
                sp.sem_inc(out_stored_dve, 1)

            def next_batch(b):
                sp.wait_ge(inputs_read, 1)
                sp.sem_inc(inputs_read, -1)
                load_batch(b)

            load_batch(0)
            next_batch(1)
            with sp.Fori(1, BATCH - 1) as i:
                next_batch(i + 1)
                store_batch(i - 1)
            store_batch(BATCH - 2)
            store_batch(BATCH - 1)

        @block.tensor
        def _(pe):
            pe.wait_ge(loaded, 16 * 18)
            sources = [w_nat[:, n, :] for n in range(4)] + [wq_nat[:, n, :] for n in range(2 * RH)]
            sources += [keys_nat[:, g, s, :] for g in range(2) for s in range(2)]
            sources += [down_nat[:, c, :] for c in range(CHUNKS)]
            for n, src in enumerate(sources):
                mm = pe.transpose(banks[n // 4][:, (n % 4) * P:(n % 4 + 1) * P], src, ident[:])
                if n % 4 == 3:
                    mm.then_inc(setup_pe, 1)
            pe.wait_ge(setup_act, 8)
            for h in range(RH):
                for s in range(2):
                    at = (2 * h + s) * NK
                    mm = pe.matmul(banks[0][:, at:at + NK], wqT[:, 2 * h + s, :],
                                   keysT[:, h // 4, s, (h % 4) * NK:(h % 4 + 1) * NK], start=True, stop=True)
            mm.then_inc(setup_pe, 1)
            pe.wait_ge(setup_act, 11)

            def iteration(attend, route):
                plan, used, _ = misc_plan(attend, route)

                def take(name):
                    b, before, _, _ = plan[name]
                    if before:
                        pe.wait_ge(misc_read[b], before)
                    return misc_ps[b]

                def give(mm, name):
                    b, _, _, reader = plan[name]
                    mm.then_inc(misc_for[b, reader], 1)

                def was_read(name):
                    b, before, _, _ = plan[name]
                    pe.wait_ge(misc_read[b], before + 1)

                def hidden():
                    for n in range(4):
                        ps = take(f"hidden{n}")
                        for c in (2 * n, 2 * n + 1):
                            mm = pe.matmul(ps[:, (c % 2) * SEQ:(c % 2 + 1) * SEQ], downT[:, c, :], xnT[:],
                                           start=True, stop=True)
                        give(mm, f"hidden{n}")

                def project():
                    ps = take("ctxT")
                    pe.wait_ge(ctx_loaded, 32)
                    give(pe.transpose(ps[:, 0:P], ctx_in[:], ident[:]), "ctxT")
                    ps = take("yT")
                    pe.wait_ge(y_ready, 1)
                    for t in range(TILES):
                        mm = pe.transpose(ps[:, t * P:(t + 1) * P], y[:, t, :], ident[:])
                    give(mm, "yT")
                    ps = take("qkv")
                    was_read("ctxT")
                    pe.matmul(ps[:, SEQ:SEQ + CTX], wT[:, 1, :], ctxT[:, 0:CTX], start=True, stop=True)
                    pe.matmul(ps[:, SEQ + CTX:SEQ + CTX + D], ctxT[:], wT[:, 2, :], start=True, stop=True)
                    was_read("yT")
                    give(pe.matmul(ps[:, 0:SEQ], wT[:, 0, :], yT[:], start=True, stop=True), "qkv")

                def score(t):
                    was_read("qkv")
                    pe.wait_ge(k_blocks_ready, 1)
                    for s in range(2):
                        ps = take(f"scores{t}{s}")
                        give(pe.matmul(ps[:], qT[:, t * P:(t + 1) * P],
                                       k_blocks[:, s * 8:(s + 1) * 8, :].rearrange("p h k -> p (h k)"),
                                       start=True, stop=True), f"scores{t}{s}")

                def turn_probs(t):
                    pe.wait_ge(shifted, t + 1)
                    flat = scores[:, t, :, :].rearrange("p h k -> p (h k)")
                    for s in range(2):
                        ps = take(f"probsT{t}{s}")
                        for c in range(4):
                            at = (4 * s + c) * P
                            mm = pe.transpose(ps[:, c * P:(c + 1) * P], flat[:, at:at + P], ident[:])
                        give(mm, f"probsT{t}{s}")

                def attend_values(t):
                    ps = take(f"attn{t}")
                    pe.wait_ge(v_blocks_ready, 1)
                    was_read(f"probsT{t}0")
                    was_read(f"probsT{t}1")
                    w = 2 * (DK + 1)
                    for c in range(PAIRS):
                        mm = pe.matmul(ps[:, c * w:(c + 1) * w], probsT[:, t, c, :],
                                       v_blocks[:, c, :, :].rearrange("p a d -> p (a d)"), start=True, stop=True)
                    give(mm, f"attn{t}")

                def turn_attn(t):
                    ps = take(f"attnT{t}")
                    was_read(f"attn{t}")
                    give(pe.transpose(ps[:, 0:P], attn[:, t, :], ident[:]), f"attnT{t}")

                def project_out():
                    ps = take("proj")
                    for t in range(TILES):
                        was_read(f"attnT{t}")
                        mm = pe.matmul(ps[:, t * D:(t + 1) * D], attnT[:, t, :], wT[:, 3, :], start=True, stop=True)
                    give(mm, "proj")

                def turn_norm():
                    ps = take("normT")
                    pe.wait_ge(xn_ready, 1)
                    for t in range(TILES):
                        mm = pe.transpose(ps[:, t * P:(t + 1) * P], xn[:, t, :], ident[:])
                    give(mm, "normT")

                def similarities(t):
                    ps = take(f"sims{t}")
                    was_read("normT")
                    give(pe.matmul(ps[:], xnT[:, t * P:(t + 1) * P], sim_w[:], start=True, stop=True), f"sims{t}")

                def turn_sims(t):
                    pe.wait_ge(sims_split, t + 1)
                    for s in range(2):
                        ps = take(f"simsT{t}{s}")
                        for k in range(4):
                            src = sims_hl[:, t, 4 * s + k, :, :].rearrange("p a b -> p (a b)").bitcast(F32)
                            mm = pe.transpose(ps[:, k * P:(k + 1) * P], src, ident[:])
                        give(mm, f"simsT{t}{s}")

                def kept(t, h):
                    act = on_act(h)
                    pe.wait_ge(kept_by_act if act else kept_by_dve, 2 * heads_before(t, h, act) + 2)

                def pairs(t, h):
                    if h >= 2:
                        kept(t, h - 2)
                    for s in range(2):
                        if h % 4 == 0 and s == 0:
                            was_read(f"simsT{t}{h // 4}")
                        ps = pair_ps[2 * (h % 2) + s]
                        pe.matmul(ps[:], simsT[:, t, h, :], spread_r[:, s * HALF:(s + 1) * HALF],
                                  start=True, stop=not on_act(h), skip_group_check=True).then_inc(pairs_ready, 1)

                def lower(t, h):
                    n = heads_before(t, h, True)
                    for s in range(2):
                        pe.wait_ge(below_ready, 2 * n + s + 1)
                        pe.matmul(pair_ps[2 * (h % 2) + s][:], neg_ident[:], below[:, n % 2, s, :],
                                  start=False, stop=True, skip_group_check=True).then_inc(lowered, 1)

                def gather(t, h):
                    kept(t, h)
                    act = on_act(h)
                    n = heads_before(t, h, act)
                    buf = kept_a[:, n % ACT_SLOTS] if act else kept_d[:, n % DVE_SLOTS]
                    for s in range(2):
                        if h == 0 and t > 0:
                            pe.wait_ge(gated, 2 * (t - 1) + s + 1)
                        for c in range(4):
                            mm = pe.matmul(score_ps[s][:, c * P:(c + 1) * P], buf[:, s, c * P:(c + 1) * P], ident[:],
                                           is_transpose=True, start=(h == 0 and c == 0), stop=(h == RH - 1),
                                           skip_group_check=True)
                        if h == RH - 1:
                            mm.then_inc(score_ready, 1)
                    if h < RH - 1:
                        mm.then_inc(kept_a_read if act else kept_d_read, 1)

                def mix(t):
                    ps = take(f"out{t}")
                    pe.wait_ge(gated, 2 * t + 2)
                    for c in range(CHUNKS):
                        mm = pe.matmul(ps[:, 0:D], gatedT[:, c, :], up_sb[:, c, :],
                                       start=(c == 0), stop=(c == CHUNKS - 1))
                    give(mm, f"out{t}")

                def head(t, h):
                    pairs(t, h)
                    if h >= 1 and on_act(h - 1):
                        lower(t, h - 1)
                    if h >= 2:
                        gather(t, h - 2)

                def last_heads(t):
                    if on_act(RH - 1):
                        lower(t, RH - 1)
                    gather(t, RH - 2)
                    gather(t, RH - 1)

                if route:
                    hidden()
                if attend:
                    project()
                    for t in range(TILES):
                        score(t)
                if route:
                    turn_sims(0)
                for h in range(RH):
                    if route:
                        head(0, h)
                    if attend:
                        if h == 1:
                            turn_probs(0)
                        if h == 3:
                            attend_values(0)
                            turn_probs(1)
                        if h == 5:
                            attend_values(1)
                        if h == 6:
                            turn_attn(0)
                            turn_attn(1)
                        if h == 7:
                            project_out()
                if route:
                    last_heads(0)
                    turn_sims(1)
                    mix(0)
                for h in range(RH):
                    if route:
                        head(1, h)
                    if attend:
                        if h == 2:
                            turn_norm()
                        if h == 3:
                            similarities(0)
                        if h == 4:
                            similarities(1)
                if route:
                    last_heads(1)
                    mix(1)

                for b in range(2):
                    pe.wait_ge(misc_read[b], used[b])
                pe.drain()
                for b in range(2):
                    pe.sem_inc(misc_read[b], -used[b])
                if attend:
                    pe.sem_inc(ctx_loaded, -32)
                    pe.sem_inc(y_ready, -1)
                    pe.sem_inc(k_blocks_ready, -1)
                    pe.sem_inc(v_blocks_ready, -1)
                    pe.sem_inc(shifted, -TILES)
                    pe.sem_inc(xn_ready, -1)
                if route:
                    pe.sem_inc(sims_split, -TILES)
                    pe.sem_inc(kept_by_dve, -2 * TILES * (RH - len(ACT_HEADS)))
                    pe.sem_inc(kept_by_act, -2 * TILES * len(ACT_HEADS))
                    pe.sem_inc(below_ready, -2 * TILES * len(ACT_HEADS))
                    pe.sem_inc(gated, -2 * TILES)

            iteration(True, False)
            with pe.Fori(1, BATCH):
                iteration(True, True)
            iteration(False, True)

        @block.scalar
        def _(act):
            act.wait_ge(loaded, 16 * 18)
            nc.scalar.activation(spread_r[:], spread_f[:], ACT.Identity)
            nc.scalar.activation(neg_ident[:], ident[:], ACT.Identity, scale=-1.0)
            nc.scalar.activation(bk_scaled[:], bk[:], ACT.Identity, scale=float(DK) ** -0.5)
            targets = [wT[:]] + [wqT[:, 4 * n:4 * n + 4, :] for n in range(4)]
            targets += [keysT[:].rearrange("p g s k -> p (g s) k")]
            targets += [downT[:, 4 * n:4 * n + 4, :] for n in range(2)]
            for n, dst in enumerate(targets):
                act.wait_ge(setup_pe, n + 1)
                src = banks[n][:].rearrange("p (a b) -> p a b", a=4)
                if n >= 6:
                    nc.scalar.activation(dst, src, ACT.Copy, scale=nw[:, 0:1]).then_inc(setup_act, 1)
                else:
                    nc.scalar.activation(dst, src, ACT.Copy).then_inc(setup_act, 1)
            act.wait_ge(setup_pe, 9)
            nc.scalar.activation(sim_w[:], banks[0][:], ACT.Copy, scale=nw[:, 0:1]).then_inc(setup_act, 3)

            def iteration(attend, route):
                plan, _, read = misc_plan(attend, route)

                def take(name):
                    b, _, k, _ = plan[name]
                    act.wait_ge(misc_for[b, "act"], k + 1)
                    return misc_ps[b], misc_read[b]

                def keep(t, h):
                    n = heads_before(t, h, True)
                    if n >= ACT_SLOTS:
                        act.wait_ge(kept_a_read, n - ACT_SLOTS + 1)
                    for s in range(2):
                        act.wait_ge(pairs_ready, 2 * (t * RH + h) + s + 1)
                        nc.scalar.activation(below[:, n % 2, s, :], pair_ps[2 * (h % 2) + s][:], ACT.Relu,
                                             scale=-STEEP, bias=steep_cut[:, t, h:h + 1]).then_inc(below_ready, 1)
                    for s in range(2):
                        act.wait_ge(lowered, 2 * n + s + 1)
                        nc.scalar.activation(kept_a[:, n % ACT_SLOTS, s, :], pair_ps[2 * (h % 2) + s][:],
                                             ACT.Relu).then_inc(kept_by_act, 1)

                def copy_pairs(t, h):
                    n = heads_before(t, h, False)
                    for s in range(2):
                        act.wait_ge(pairs_ready, 2 * (t * RH + h) + s + 1)
                        nc.scalar.activation(pair_sums[:, n % 2, s, :], pair_ps[2 * (h % 2) + s][:],
                                             ACT.Identity).then_inc(pairs_copied, 1)

                def turn_sims(t):
                    for s in range(2):
                        ps, done = take(f"simsT{t}{s}")
                        nc.scalar.activation(simsT[:, t, 4 * s:4 * s + 4, :],
                                             ps[:].rearrange("p (a b) -> p a b", a=4), ACT.Identity).then_inc(done, 1)

                def exps(t):
                    for s in range(2):
                        ps, done = take(f"probsT{t}{s}")
                        nc.scalar.activation(probsT[:, t, 4 * s:4 * s + 4, :],
                                             ps[:].rearrange("p (a b) -> p a b", a=4), ACT.Exp).then_inc(done, 1)

                if route:
                    for n in range(4):
                        ps, done = take(f"hidden{n}")
                        nc.scalar.activation(geluT[:, 2 * n:2 * n + 2, :], ps[:].rearrange("p (a b) -> p a b", a=2),
                                             ACT.Gelu).then_inc(done, 1)
                    nc.scalar.copy(flag[:, 0:1], ident[:, 0:1]).then_inc(gelu_ready, 1)
                if attend:
                    ps, done = take("ctxT")
                    nc.scalar.activation(ctxT[:], ps[:, 0:P], ACT.Identity).then_inc(done, 1)
                    ps, done = take("yT")
                    nc.scalar.activation(yT[:], ps[:, 0:SEQ], ACT.Identity).then_inc(done, 1)
                    ps, done = take("qkv")
                    nc.scalar.activation(kT[:], ps[:, SEQ:SEQ + CTX], ACT.Identity,
                                         scale=float(DK) ** -0.5, bias=bk_scaled[:, 0:1])
                    nc.scalar.activation(v_in[:], ps[:, SEQ + CTX:SEQ + CTX + D], ACT.Identity).then_inc(v_ready, 1)
                    nc.scalar.activation(qT[:], ps[:, 0:SEQ], ACT.Identity, bias=bq[:, 0:1]).then_inc(done, 1)
                    for t in range(TILES):
                        for s in range(2):
                            ps, done = take(f"scores{t}{s}")
                            nc.scalar.activation(
                                scores[:, t, 8 * s:8 * s + 8, :], ps[:].rearrange("p (h k) -> p h k", h=8),
                                ACT.Identity).then_inc(done, 1)
                        nc.scalar.copy(flag[:, 1 + t:2 + t], ident[:, 0:1]).then_inc(scores_ready, 1)
                if route:
                    turn_sims(0)
                for h in range(RH):
                    if route and on_act(h):
                        if h == ACT_HEADS[0]:
                            act.wait_ge(cut_ready, 1)
                        keep(0, h)
                    elif route:
                        copy_pairs(0, h)
                    if attend:
                        if h == 1:
                            exps(0)
                        if h == 3:
                            exps(1)
                        if h == 6:
                            for t in range(TILES):
                                ps, done = take(f"attnT{t}")
                                nc.scalar.activation(attnT[:, t, :], ps[:, 0:P], ACT.Identity).then_inc(done, 1)
                if route:
                    turn_sims(1)
                    act.wait_ge(cut_ready, TILES)
                for h in range(RH):
                    if route and on_act(h):
                        keep(1, h)
                    elif route:
                        copy_pairs(1, h)
                    if attend:
                        if h == 2:
                            ps, done = take("normT")
                            nc.scalar.activation(xnT[:], ps[:, 0:SEQ], ACT.Identity).then_inc(done, 1)
                        if h in (3, 4):
                            t = h - 3
                            ps, done = take(f"sims{t}")
                            nc.scalar.activation(sims[:, t, :, :, :].rearrange("p h s k -> p (h s k)"), ps[:],
                                                 ACT.Identity).then_inc(sims_for_topk, 1)
                            nc.scalar.activation(sims_hl[:, t, :, 0, :], ps[:].rearrange("p (h k) -> p h k", h=RH),
                                                 ACT.Identity).then_inc(done, 1)
                            nc.scalar.copy(flag[:, 3 + t:4 + t], ident[:, 0:1]).then_inc(sims_to_split, 1)

                act.drain()
                for b in range(2):
                    if read.get((b, "act")):
                        act.sem_inc(misc_for[b, "act"], -read[b, "act"])
                if route:
                    act.sem_inc(cut_ready, -TILES)
                    act.sem_inc(pairs_ready, -2 * TILES * RH)
                    act.sem_inc(lowered, -2 * TILES * len(ACT_HEADS))
                    reads = TILES * sum(h < RH - 1 for h in ACT_HEADS)
                    act.wait_ge(kept_a_read, reads)
                    act.sem_inc(kept_a_read, -reads)

            iteration(True, False)
            with act.Fori(1, BATCH):
                iteration(True, True)
            iteration(False, True)

        @block.gpsimd
        def _(pool):
            nc.gpsimd.memset(neg_half[:], -0.5)
            pool.wait_ge(loaded, 16 * 18)
            nc.gpsimd.tensor_copy(v_blocks[:, :, :, DK],
                                  pair_mask[:].unsqueeze(1).to_broadcast([P, PAIRS, 2]))
            pool.drain()

            def iteration(attend, route):
                steps = [0]

                def inverse_root(dst, tmp, var, scale, shift):
                    nc.gpsimd.tensor_scalar(tmp[:], var, scale, shift, ALU.mult, ALU.add).then_inc(pool_step, 1)
                    steps[0] += 1
                    pool.wait_ge(pool_step, steps[0])
                    nc.gpsimd.tensor_tensor(dst[:], tmp[:], neg_half[:], ALU.pow).then_inc(rstd_ready, 1)

                def pair_cands(t, q):
                    pool.wait_ge(halves_sorted, 2 * t + q + 1)
                    hs = slice(4 * q, 4 * q + 4)
                    at = 0
                    for i0, ni, nj in RECTS:
                        a = sorted16[:, t, hs, 0, i0:i0 + ni].unsqueeze(3).to_broadcast([P, 4, ni, nj])
                        b = sorted16[:, t, hs, 1, 0:nj].unsqueeze(2).to_broadcast([P, 4, ni, nj])
                        dst = cands[:, t, hs, at:at + ni * nj].rearrange("p h (i j) -> p h i j", i=ni)
                        last = nc.gpsimd.tensor_tensor(dst, a, b, ALU.add)
                        at += ni * nj
                    last.then_inc(cands_ready, 1)

                def blocks():
                    pool.wait_ge(v_ready, 1)
                    shape = [P, HEADS, CTX]
                    nc.gpsimd.tensor_tensor(k_blocks[:], kT[:].unsqueeze(1).to_broadcast(shape),
                                            mask[:].unsqueeze(2).to_broadcast(shape), ALU.mult).then_inc(k_blocks_ready, 1)
                    nc.gpsimd.tensor_tensor(v_biased[:], v_in[:], bv[:], ALU.add).then_inc(pool_step, 1)
                    steps[0] += 1
                    pool.wait_ge(pool_step, steps[0])
                    nc.gpsimd.tensor_tensor(v_blocks[:, :, :, 0:DK],
                                            v_biased[:].rearrange("p (c a d) -> p c a d", a=2, d=DK),
                                            pair_mask[:].unsqueeze(1).unsqueeze(3).to_broadcast([P, PAIRS, 2, DK]),
                                            ALU.mult).then_inc(v_blocks_ready, 1)
                    nc.gpsimd.memset(pool_mark[:], 0.0).then_inc(inputs_read, 1)

                def shift_scores(t):
                    pool.wait_ge(peak_ready, t + 1)
                    nc.gpsimd.tensor_tensor(scores[:, t], scores[:, t],
                                            peak[:, t, :].unsqueeze(2).to_broadcast([P, HEADS, CTX]),
                                            ALU.subtract).then_inc(shifted, 1)

                if attend:
                    pool.wait_ge(var_ready, 1)
                    inverse_root(rstd, shifted_var, mean_var[:, :, 1], 1.0, EPS)
                    for t in range(TILES):
                        last = nc.gpsimd.tensor_tensor(x_bias[:, t, :], x_in[:, t, :], bo[:], ALU.add)
                if route:
                    pair_cands(0, 0)
                if attend:
                    blocks()
                if route:
                    pair_cands(0, 1)
                if attend:
                    for t in range(TILES):
                        shift_scores(t)
                if route:
                    pair_cands(1, 0)
                    pair_cands(1, 1)
                if attend:
                    pool.wait_ge(var_ready, 2)
                    inverse_root(rstd2, shifted_var2, mean_var2[:, :, 1], 1.0 + EPS, EPS * EPS)
                    for t in range(TILES):
                        pool.wait_ge(sims_to_split, t + 1)
                        nc.gpsimd.tensor_tensor(
                            sims_hl[:, t, :, 1, :], sims[:, t, :, :, :].rearrange("p h s k -> p h (s k)"),
                            sims_hl[:, t, :, 0, :].bitcast(F32), ALU.subtract).then_inc(sims_split, 1)

                pool.drain()
                if attend:
                    pool.sem_inc(pool_step, -steps[0])
                    pool.sem_inc(var_ready, -2)
                    pool.sem_inc(v_ready, -1)
                    pool.sem_inc(peak_ready, -TILES)
                    pool.sem_inc(sims_to_split, -TILES)
                if route:
                    pool.sem_inc(halves_sorted, -2 * TILES)

            iteration(True, False)
            with pool.Fori(1, BATCH):
                iteration(True, True)
            iteration(False, True)

        @block.vector
        def _(dve):
            dve.wait_ge(loaded, 16 * 18)

            def iteration(attend, route, free_out):
                plan, _, read = misc_plan(attend, route)
                steps = [0]

                def step(ins):
                    ins.then_inc(dve_step, 1)
                    steps[0] += 1
                    return steps[0]

                def take(name):
                    b, _, k, _ = plan[name]
                    dve.wait_ge(misc_for[b, "dve"], k + 1)
                    return misc_ps[b], misc_read[b]

                def variance(src, st, mv):
                    for t in range(TILES):
                        n = step(nc.vector.bn_stats(st[:, t, :], src[:, t, :]))
                    dve.wait_ge(dve_step, n)
                    nc.vector.bn_aggr(mv[:, 0, :], st[:, 0, :])
                    nc.vector.bn_aggr(mv[:, 1, :], st[:, 1, :]).then_inc(var_ready, 1)

                def normalise(dst, src, mv, r, ready):
                    for t in range(TILES):
                        last = nc.vector.tensor_scalar(dst[:, t, :], src[:, t, :], mv[:, t, 0:1], r[:, t:t + 1],
                                                       ALU.subtract, ALU.mult)
                    last.then_inc(ready, 1)

                def sort_halves(t, q):
                    lists = [(h, s) for h in range(4 * q, 4 * q + 4) for s in range(2)]
                    first = [step(nc.vector.max(sorted16[:, t, h, s, 0:8], sims[:, t, h, s, :])) for h, s in lists]
                    taken = []
                    for (h, s), n in zip(lists, first):
                        dve.wait_ge(dve_step, n)
                        taken.append(step(nc.vector.match_replace(
                            rest[:, t, h, s, :], sorted16[:, t, h, s, 0:8], sims[:, t, h, s, :], LOWEST)))
                    for (h, s), n in zip(lists, taken):
                        dve.wait_ge(dve_step, n)
                        last = nc.vector.max(sorted16[:, t, h, s, 8:16], rest[:, t, h, s, :])
                    last.then_inc(halves_sorted, 1)

                def find_best(t, q):
                    dve.wait_ge(cands_ready, 2 * t + q + 1)
                    hs = range(4 * q, 4 * q + 4)
                    first = [step(nc.vector.max(best[:, t, h, 0:8], cands[:, t, h, :])) for h in hs]
                    taken = []
                    for h, n in zip(hs, first):
                        dve.wait_ge(dve_step, n)
                        taken.append(step(nc.vector.match_replace(
                            cands_rest[:, t, h, :], best[:, t, h, 0:8], cands[:, t, h, :], LOWEST)))
                    for h, n in zip(hs, taken):
                        dve.wait_ge(dve_step, n)
                        n = step(nc.vector.max(best[:, t, h, 8:16], cands_rest[:, t, h, :]))
                    return n

                def set_cut(t, n):
                    m = step(nc.vector.tensor_tensor(top_sim[:, t, :], sorted16[:, t, :, 0, 0], sorted16[:, t, :, 1, 0],
                                                     ALU.max))
                    dve.wait_ge(dve_step, max(m, n))
                    n = step(nc.vector.scalar_tensor_tensor(cut_raw[:, t, :], top_sim[:, t, :], -MARGIN,
                                                            best[:, t, :, TOP - 1], ALU.mult, ALU.add))
                    dve.wait_ge(dve_step, n)
                    n = step(nc.vector.tensor_scalar(cut[:, t, :], cut_raw[:, t, :], TINY, None, ALU.max))
                    dve.wait_ge(dve_step, n)
                    nc.vector.tensor_scalar(steep_cut[:, t, :], cut[:, t, :], STEEP, None, ALU.mult).then_inc(cut_ready, 1)

                def find_peak(t):
                    dve.wait_ge(scores_ready, t + 1)
                    nc.vector.tensor_reduce(peak[:, t, :], scores[:, t], AX.X, ALU.max).then_inc(peak_ready, 1)

                def keep(t, h):
                    n = heads_before(t, h, False)
                    if n >= DVE_SLOTS:
                        dve.wait_ge(kept_d_read, n - DVE_SLOTS + 1)
                    for s in range(2):
                        dve.wait_ge(pairs_copied, 2 * n + s + 1)
                        z = pair_sums[:, n % 2, s, :]
                        nc.vector.scalar_tensor_tensor(kept_d[:, n % DVE_SLOTS, s, :], z, cut[:, t, h:h + 1], z,
                                                       ALU.is_ge, ALU.mult).then_inc(kept_by_dve, 1)

                def divide(t):
                    ps, done = take(f"attn{t}")
                    v = ps[:, 0:HEADS * (DK + 1)].rearrange("p (h d) -> p h d", d=DK + 1)
                    n = step(nc.vector.reciprocal(rsum[:, t, :], v[:, :, DK]))
                    dve.wait_ge(dve_step, n)
                    nc.vector.tensor_tensor(attn[:, t, :].rearrange("p (h d) -> p h d", d=DK), v[:, :, 0:DK],
                                            rsum[:, t, :].unsqueeze(2).to_broadcast([P, HEADS, DK]),
                                            ALU.mult).then_inc(done, 1)

                def residual():
                    ps, done = take("proj")
                    n = step(nc.vector.tensor_tensor(x1_new[:, 0, :], ps[:, 0:D], x_bias[:, 0, :], ALU.add))
                    nc.vector.tensor_tensor(x1_new[:, 1, :], ps[:, D:2 * D], x_bias[:, 1, :], ALU.add).then_inc(done, 1)
                    dve.wait_ge(dve_step, n)
                    n = step(nc.vector.bn_stats(stats2[:, 0, :], x1_new[:, 0, :]))
                    dve.wait_ge(dve_step, n)
                    n = step(nc.vector.bn_stats(stats2[:, 1, :], x1_new[:, 1, :]))
                    dve.wait_ge(dve_step, n)
                    nc.vector.bn_aggr(mean_var2[:, 0, :], stats2[:, 0, :])
                    nc.vector.bn_aggr(mean_var2[:, 1, :], stats2[:, 1, :]).then_inc(var_ready, 1)

                def gate(t):
                    if t == 0:
                        dve.wait_ge(gelu_ready, 1)
                    for s in range(2):
                        dve.wait_ge(score_ready, 2 * t + s + 1)
                        nc.vector.tensor_tensor(gatedT[:, 4 * s:4 * s + 4, :],
                                                score_ps[s][:].rearrange("p (c t) -> p c t", c=4),
                                                geluT[:, 4 * s:4 * s + 4, t * P:(t + 1) * P],
                                                ALU.mult).then_inc(gated, 1)

                def finish(t):
                    if t == 0 and free_out:
                        dve.wait_ge(out_stored_dve, 1)
                    ps, done = take(f"out{t}")
                    nc.vector.tensor_tensor(y_out[:, t, :], ps[:, 0:D], x1[:, t, :], ALU.add).then_inc(done, 1)
                    nc.vector.memset(mark[:, t:t + 1], 0.0).then_inc(out_ready, 1)

                if route:
                    n = step(nc.vector.tensor_copy(x1[:], x1_new[:]))
                if attend:
                    dve.wait_ge(x_loaded, 16)
                    variance(x_in, stats, mean_var)
                if route:
                    dve.wait_ge(sims_for_topk, 1)
                    sort_halves(0, 0)
                if attend:
                    dve.wait_ge(rstd_ready, 1)
                    normalise(y, x_in, mean_var, rstd, y_ready)
                if route:
                    sort_halves(0, 1)
                    find_best(0, 0)
                if attend:
                    find_peak(0)
                if route:
                    set_cut(0, find_best(0, 1))
                if attend:
                    find_peak(1)
                if route:
                    dve.wait_ge(sims_for_topk, 2)
                for h in range(RH):
                    if route and not on_act(h):
                        keep(0, h)
                    if route:
                        if h == 1:
                            sort_halves(1, 0)
                        if h == 3:
                            sort_halves(1, 1)
                        if h == 5:
                            find_best(1, 0)
                        if h == 6:
                            set_cut(1, find_best(1, 1))
                    if attend:
                        if h == 4:
                            divide(0)
                        if h == 6:
                            divide(1)
                if route:
                    gate(0)
                if attend:
                    residual()
                for h in range(RH):
                    if route and not on_act(h):
                        keep(1, h)
                    if h == 1 and attend:
                        dve.wait_ge(rstd_ready, 2)
                        normalise(xn, x1_new, mean_var2, rstd2, xn_ready)
                    if h == 0 and route:
                        finish(0)
                if route:
                    gate(1)
                    finish(1)

                dve.drain()
                dve.sem_inc(dve_step, -steps[0])
                for b in range(2):
                    if read.get((b, "dve")):
                        dve.sem_inc(misc_for[b, "dve"], -read[b, "dve"])
                if attend:
                    dve.sem_inc(x_loaded, -16)
                    dve.sem_inc(rstd_ready, -2)
                    dve.sem_inc(scores_ready, -TILES)
                if route:
                    dve.sem_inc(sims_for_topk, -TILES)
                    dve.sem_inc(cands_ready, -2 * TILES)
                    dve.sem_inc(pairs_copied, -2 * TILES * (RH - len(ACT_HEADS)))
                    reads = TILES * sum(not on_act(h) for h in range(RH - 1))
                    dve.wait_ge(kept_d_read, reads)
                    dve.sem_inc(kept_d_read, -reads)
                    dve.sem_inc(score_ready, -2 * TILES)
                    dve.sem_inc(gelu_ready, -1)
                    if free_out:
                        dve.sem_inc(out_stored_dve, -1)

            iteration(True, False, False)
            iteration(True, True, False)
            with dve.Fori(2, BATCH):
                iteration(True, True, True)
            iteration(False, True, True)


_INS = [("x", "x"), ("ctx_1024", "ctx"), ("L0_xattn_W_Q", "W_Q"), ("L0_xattn_b_Q", "b_Q"), ("L0_xattn_W_K", "W_K"),
        ("L0_xattn_b_K", "b_K"), ("L0_xattn_W_V", "W_V"), ("L0_xattn_b_V", "b_V"), ("L0_xattn_W_O", "W_O"),
        ("L0_xattn_b_O", "b_O"), ("L0_ffn_norm_w", "norm_w"), ("L0_ffn_wq", "wq"), ("L0_ffn_keys", "keys"),
        ("L0_ffn_expert_down", "down"), ("L0_ffn_expert_up", "up")]


def kernel(**inputs):
    import numpy as np
    import concourse.bacc as bacc
    from concourse import mybir as mb
    from concourse.bass_utils import run_bass_kernel_spmd

    arrays = {f"in_{short}": np.ascontiguousarray(inputs[name]) for name, short in _INS}
    arrays["in_eye"] = np.eye(P, dtype=np.float32)
    row, col = np.arange(P)[:, None] % (2 * NK), np.arange(EXPERTS)[None, :]
    arrays["in_spread"] = ((row == col // NK) | (row == NK + col % NK)).astype(np.float32)
    arrays["in_head_mask"] = (np.arange(P)[:, None] // DK == np.arange(HEADS)[None, :]).astype(np.float32)
    arrays["in_key_mask"] = (np.arange(P)[:, None] // CTX == np.arange(2)[None, :]).astype(np.float32)

    nc = bacc.Bacc("TRN2", target_bir_lowering=False, num_devices=1)
    aps = [nc.dram_tensor(n, a.shape, mb.dt.from_np(a.dtype), kind="ExternalInput").ap() for n, a in arrays.items()]
    out = nc.dram_tensor("out", (BATCH, SEQ, D), mb.dt.float32, kind="ExternalOutput").ap()
    xattn_peer_kernel(nc, *aps, out)
    r = run_bass_kernel_spmd(nc, [arrays], core_ids=[0])
    return r.results[0]["out"]
```

```python
from contextlib import ExitStack

import concourse.bass as bass
from concourse import mybir

ALU = mybir.AluOpType
ACT = mybir.ActivationFunctionType
AX = mybir.AxisListType
F32 = mybir.dt.float32
F32R = mybir.dt.float32r
BF16 = mybir.dt.bfloat16

P = 128
D = 128
BATCH, SEQ, CTX = 16, 256, 64
TILES = SEQ // P
HEADS, DK = 16, 8
PAIRS = HEADS // 2
EPS = 1e-5
RH, NK, TOP = 8, 32, 16
EXPERTS = NK * NK
CHUNKS = EXPERTS // P
HALF = 512
LOWEST = -3.0e38
TINY = 1e-37
STEEP = float(2 ** 30)
MARGIN = float(2 ** -20)

RECTS = [(0, 1, 16), (1, 1, 8), (2, 2, 5), (4, 4, 3), (8, 8, 1)]
CANDS = sum(n * m for _, n, m in RECTS)

ACT_HEADS = (1, 4, 6)
DVE_HEADS = tuple(h for h in range(RH) if h not in ACT_HEADS)
assert RH - 1 in DVE_HEADS and len(ACT_HEADS) == 3 and RH - 2 in ACT_HEADS

ITEMS = TILES * RH
PAIR_BUF = [g % 3 for g in range(ITEMS - 1)] + [1]


def pair_buf(g):
    return PAIR_BUF[g % ITEMS]


def user_before(g):
    n = g - 1
    while pair_buf(n) != pair_buf(g):
        n -= 1
    return n


def count_items(kind, first, last):
    return sum(g % RH in kind for g in range(first, last + 1))


SHARED = [
    (0, "route", "simsT10", "act"), (0, "route", "simsT11", "act"),
    (1, "late", "attnT", "act"), (1, "tail", "kept10", "dve"), (1, "tail", "kept11", "dve"),
    (2, "late", "proj", "dve"), (2, "early", "inputsT", "act"), (2, "tail", "out1", "dve"),
    (3, "route", "hidden0", "act"),
    (4, "early", "qkv", "act"), (4, "route", "hidden1", "act"),
    (5, "route", "hidden2", "act"), (5, "route", "hidden3", "act"),
    (6, "late", "normT", "act"), (6, "early", "scores00", "act"), (6, "early", "scores01", "act"),
    (7, "late", "sims0", "act"), (7, "late", "sims1", "act"),
    (8, "early", "scores10", "act"), (8, "early", "scores11", "act"),
    (9, "route", "kept00", "dve"), (9, "route", "kept01", "dve"),
    (10, "early", "probsT00", "act"), (10, "early", "probsT01", "act"),
    (11, "late", "simsT00", "act"),
    (12, "early", "probsT10", "act"), (12, "early", "probsT11", "act"), (12, "early", "attn0", "dve"),
    (13, "late", "simsT01", "act"), (13, "route", "out0", "dve"),
    (14, "early", "attn1", "dve"),
]


def misc_plan(tail, route, late, early):
    on = {"tail": tail, "route": route, "late": late, "early": early}
    order = [(name, reader) for _, stage, name, reader in SHARED if on[stage]]
    plan, used, read = {}, [0, 0], {}
    for n, (name, reader) in enumerate(order):
        b = n % 2
        k = read.get((b, reader), 0)
        plan[name] = (b, used[b], k, reader)
        used[b] += 1
        read[(b, reader)] = k + 1
    return plan, used, read


def xattn_peer_kernel(nc, x, ctx, W_Q, b_Q, W_K, b_K, W_V, b_V, W_O, b_O,
                      norm_w, wq, keys, down, up, eye, spread, head_mask, key_mask, out):
    with ExitStack() as stack:
        def sb(name, shape, dt=F32):
            return stack.enter_context(nc.sbuf_tensor(name, shape, dt))

        def sem(name):
            return stack.enter_context(nc.semaphore(name))

        ident = sb("ident", [P, P])
        neg_ident = sb("neg_ident", [P, P], BF16)
        spread_f = sb("spread_f", [P, EXPERTS])
        spread_r = sb("spread_r", [P, EXPERTS], F32R)
        mask = sb("mask", [P, HEADS])
        pair_mask = sb("pair_mask", [P, 2])
        pool_mark = sb("pool_mark", [P, 1])
        v_biased = sb("v_biased", [P, D])
        w_nat = sb("w_nat", [P, 4, D])
        wT = sb("wT", [P, 4, D])
        bq = sb("bq", [P, 1])
        bk = sb("bk", [P, 1])
        bk_scaled = sb("bk_scaled", [P, 1])
        bv = sb("bv", [P, D])
        bo = sb("bo", [P, D])
        nw = sb("nw", [P, 1])
        wq_nat = sb("wq_nat", [P, 2 * RH, P])
        wqT = sb("wqT", [P, 2 * RH, P])
        keys_nat = sb("keys_nat", [P, 2, 2, P])
        keysT = sb("keysT", [P, 2, 2, P])
        sim_w = sb("sim_w", [P, RH * 2 * NK])
        down_nat = sb("down_nat", [P, CHUNKS, D])
        downT = sb("downT", [P, CHUNKS, P])
        up_sb = sb("up_sb", [P, CHUNKS, D])
        neg_half = sb("neg_half", [P, TILES])

        x_in = sb("x_in", [P, TILES, D])
        ctx_in = sb("ctx_in", [P, D])
        x_bias = sb("x_bias", [P, TILES, D])
        stats = sb("stats", [P, TILES, 6])
        mean_var = sb("mean_var", [P, TILES, 2])
        stats2 = sb("stats2", [P, TILES, 6])
        mean_var2 = sb("mean_var2", [P, TILES, 2])
        shifted_var = sb("shifted_var", [P, TILES])
        rstd = sb("rstd", [P, TILES])
        shifted_var2 = sb("shifted_var2", [P, TILES])
        rstd2 = sb("rstd2", [P, TILES])
        y = sb("y", [P, TILES, D])
        yT = sb("yT", [P, SEQ])
        ctxT = sb("ctxT", [P, P])
        qT = sb("qT", [P, SEQ])
        kT = sb("kT", [P, CTX])
        v_in = sb("v_in", [P, D])
        k_blocks = sb("k_blocks", [P, HEADS, CTX])
        v_blocks = sb("v_blocks", [P, PAIRS, 2, DK + 1])
        scores = sb("scores", [P, TILES, HEADS, CTX])
        peak = sb("peak", [P, TILES, HEADS])
        probsT = sb("probsT", [P, TILES, PAIRS, P])
        rsum = sb("rsum", [P, TILES, HEADS])
        attn = sb("attn", [P, TILES, D])
        attnT = sb("attnT", [P, TILES, P])
        x1_new = sb("x1_new", [P, TILES, D])
        x1 = sb("x1", [P, TILES, D])
        x1_tail = sb("x1_tail", [P, D])
        xn = sb("xn", [P, TILES, D])
        xnT = sb("xnT", [P, SEQ])
        flag = sb("flag", [P, 8])

        sims = sb("sims", [P, TILES, RH, 2, NK])
        sims_hl = sb("sims_hl", [P, TILES, RH, 2, 2 * NK], F32R)
        simsT = sb("simsT", [P, TILES, RH, P], F32R)
        sorted16 = sb("sorted16", [P, TILES, RH, 2, TOP])
        rest = sb("rest", [P, TILES, RH, 2, NK])
        cands = sb("cands", [P, TILES, RH, CANDS])
        cands_rest = sb("cands_rest", [P, TILES, RH, CANDS])
        best = sb("best", [P, TILES, RH, TOP])
        top_sim = sb("top_sim", [P, TILES, RH])
        cut_raw = sb("cut_raw", [P, TILES, RH])
        cut = sb("cut", [P, TILES, RH])
        steep_cut = sb("steep_cut", [P, TILES, RH])
        kept_sum = sb("kept_sum", [P, TILES, 2, HALF])
        kept_act = sb("kept_act", [P, TILES, 2, HALF])
        kept_a = sb("kept_a", [P, 2, 2, HALF])
        below = sb("below", [P, 2, 2 * HALF], BF16)
        geluT = sb("geluT", [P, CHUNKS, SEQ])
        gatedT = sb("gatedT", [P, CHUNKS, P])
        y_out = sb("y_out", [P, TILES, D])
        mark = sb("mark", [P, 8])

        pair_ps = [stack.enter_context(nc.psum_tensor(f"pair_ps{n}", [P, 2 * HALF], F32)) for n in range(3)]
        misc_ps = [stack.enter_context(nc.psum_tensor(f"misc_ps{n}", [P, HALF], F32)) for n in range(2)]
        banks = [ps[:, s * HALF:(s + 1) * HALF] for ps in pair_ps for s in range(2)] + [ps[:] for ps in misc_ps]

        loaded = sem("loaded")
        setup_dve = sem("setup_dve")
        setup_pe = sem("setup_pe")
        setup_act = sem("setup_act")
        setup_pool = sem("setup_pool")
        x_loaded = sem("x_loaded")
        ctx_loaded = sem("ctx_loaded")
        inputs_read = sem("inputs_read")
        var_ready = sem("var_ready")
        rstd_ready = sem("rstd_ready")
        y_ready = sem("y_ready")
        v_ready = sem("v_ready")
        k_blocks_ready = sem("k_blocks_ready")
        v_blocks_ready = sem("v_blocks_ready")
        scores_ready = sem("scores_ready")
        peak_ready = sem("peak_ready")
        shifted = sem("shifted")
        xn_ready = sem("xn_ready")
        sims_for_topk = [sem(f"sims{t}_for_topk") for t in range(TILES)]
        sims_to_split = sem("sims_to_split")
        sims_split = [sem(f"sims{t}_split") for t in range(TILES)]
        halves_sorted = sem("halves_sorted")
        cands_ready = sem("cands_ready")
        cut_ready = [sem(f"cut{t}_ready") for t in range(TILES)]
        pairs_ready = sem("pairs_ready")
        below_ready = sem("below_ready")
        lowered_for_act = sem("lowered_for_act")
        lowered_for_dve = sem("lowered_for_dve")
        kept_by_act = sem("kept_by_act")
        kept_by_dve = sem("kept_by_dve")
        kept_for_pool = sem("kept_for_pool")
        kept_pooled = sem("kept_pooled")
        gelu_ready = sem("gelu_ready")
        gated = sem("gated")
        out_ready = sem("out_ready")
        out_stored = sem("out_stored")
        out_free = sem("out_free")
        misc_for = {(b, e): sem(f"misc{b}_for_{e}") for b in range(2) for e in ("act", "dve")}
        misc_read = [sem(f"misc{b}_read") for b in range(2)]
        dve_step = sem("dve_step")
        pool_step = sem("pool_step")

        x_v = x.rearrange("b (t p) d -> b p t d", p=P)
        out_v = out.rearrange("b (t p) d -> b p t d", p=P)

        block = stack.enter_context(nc.Block())

        @block.sync
        def _(sp):
            loads = [
                (ident[:], eye), (w_nat[:, 0, :], W_Q), (w_nat[:, 1, :], W_K), (w_nat[:, 2, :], W_V),
                (w_nat[:, 3, :], W_O), (nw[:], norm_w.rearrange("(p o) -> p o", o=1)),
                (bq[:], b_Q.rearrange("(p o) -> p o", o=1)), (bk[:], b_K.rearrange("(p o) -> p o", o=1)),
                (wq_nat[:].rearrange("p c d -> p (c d)"), wq),
            ]
            loads += [(keys_nat[:, g, :, :], keys[4 * g:4 * g + 4].rearrange("h k s d -> (h k) s d")) for g in range(2)]
            loads += [
                (down_nat[:], down.rearrange("(c p) d -> p c d", p=P)),
                (up_sb[:], up.rearrange("(c p) d -> p c d", p=P)),
                (spread_f[:], spread), (mask[:], head_mask), (pair_mask[:], key_mask),
                (bv[:], b_V.rearrange("(o d) -> o d", o=1).to_broadcast([P, D])),
                (bo[:], b_O.rearrange("(o d) -> o d", o=1).to_broadcast([P, D])),
            ]
            for dst, src in loads:
                sp.dma_start(dst, src).then_inc(loaded, 16)
            assert len(loads) == 18

            def load_batch(b):
                sp.dma_start(x_in[:], x_v[b]).then_inc(x_loaded, 16)
                sp.dma_start(ctx_in[0:CTX, :], ctx[b]).then_inc(ctx_loaded, 16)
                sp.dma_start(ctx_in[CTX:P, :], ctx[b]).then_inc(ctx_loaded, 16)

            def store_batch(b):
                for t in range(TILES):
                    sp.wait_ge(out_ready, t + 1)
                    sp.dma_start(out_v[b, :, t, :], y_out[:, t, :]).then_inc(out_stored, 16)
                sp.sem_inc(out_ready, -TILES)
                sp.wait_ge(out_stored, 16 * TILES)
                sp.sem_inc(out_stored, -16 * TILES)
                sp.sem_inc(out_free, 1)

            def next_batch(b):
                sp.wait_ge(inputs_read, 1)
                sp.sem_inc(inputs_read, -1)
                load_batch(b)

            load_batch(0)
            next_batch(1)
            next_batch(2)
            with sp.Fori(1, BATCH - 2) as i:
                next_batch(i + 2)
                store_batch(i - 1)
            for b in range(BATCH - 3, BATCH):
                store_batch(b)

        @block.tensor
        def _(pe):
            pe.wait_ge(loaded, 16 * 18)
            sources = [w_nat[:, n, :] for n in range(4)] + [wq_nat[:, n, :] for n in range(2 * RH)]
            sources += [keys_nat[:, g, s, :] for g in range(2) for s in range(2)]
            sources += [down_nat[:, c, :] for c in range(CHUNKS)]
            for n, src in enumerate(sources):
                mm = pe.transpose(banks[n // 4][:, (n % 4) * P:(n % 4 + 1) * P], src, ident[:])
                if n % 4 == 3:
                    mm.then_inc(setup_pe, 1)
            pe.wait_ge(setup_act, 8)
            for h in range(RH):
                for s in range(2):
                    at = (2 * h + s) * NK
                    mm = pe.matmul(banks[0][:, at:at + NK], wqT[:, 2 * h + s, :],
                                   keysT[:, h // 4, s, (h % 4) * NK:(h % 4 + 1) * NK], start=True, stop=True)
            mm.then_inc(setup_pe, 1)
            pe.wait_ge(setup_act, 11)

            def iteration(tail, route, late, early):
                plan, used, _ = misc_plan(tail, route, late, early)
                first = -2 if tail else 0

                def take(name):
                    b, before, _, _ = plan[name]
                    if before:
                        pe.wait_ge(misc_read[b], before)
                    return misc_ps[b]

                def give(mm, name):
                    b, _, _, reader = plan[name]
                    mm.then_inc(misc_for[b, reader], 1)

                def was_read(name):
                    b, before, _, _ = plan[name]
                    pe.wait_ge(misc_read[b], before + 1)

                def hidden(n):
                    ps = take(f"hidden{n}")
                    for c in (2 * n, 2 * n + 1):
                        mm = pe.matmul(ps[:, (c % 2) * SEQ:(c % 2 + 1) * SEQ], downT[:, c, :], xnT[:],
                                       start=True, stop=True)
                    give(mm, f"hidden{n}")

                def turn_inputs():
                    ps = take("inputsT")
                    pe.wait_ge(ctx_loaded, 32)
                    pe.transpose(ps[:, 0:P], ctx_in[:], ident[:])
                    pe.wait_ge(y_ready, 1)
                    for t in range(TILES):
                        mm = pe.transpose(ps[:, (t + 1) * P:(t + 2) * P], y[:, t, :], ident[:])
                    give(mm, "inputsT")

                def project():
                    ps = take("qkv")
                    was_read("inputsT")
                    pe.matmul(ps[:, SEQ:SEQ + CTX], wT[:, 1, :], ctxT[:, 0:CTX], start=True, stop=True)
                    pe.matmul(ps[:, SEQ + CTX:SEQ + CTX + D], ctxT[:], wT[:, 2, :], start=True, stop=True)
                    give(pe.matmul(ps[:, 0:SEQ], wT[:, 0, :], yT[:], start=True, stop=True), "qkv")

                def score(t):
                    was_read("qkv")
                    pe.wait_ge(k_blocks_ready, 1)
                    for s in range(2):
                        ps = take(f"scores{t}{s}")
                        give(pe.matmul(ps[:], qT[:, t * P:(t + 1) * P],
                                       k_blocks[:, s * 8:(s + 1) * 8, :].rearrange("p h k -> p (h k)"),
                                       start=True, stop=True), f"scores{t}{s}")

                def turn_probs(t):
                    pe.wait_ge(shifted, t + 1)
                    flat = scores[:, t, :, :].rearrange("p h k -> p (h k)")
                    for s in range(2):
                        ps = take(f"probsT{t}{s}")
                        for c in range(4):
                            at = (4 * s + c) * P
                            mm = pe.transpose(ps[:, c * P:(c + 1) * P], flat[:, at:at + P], ident[:])
                        give(mm, f"probsT{t}{s}")

                def attend_values(t):
                    ps = take(f"attn{t}")
                    was_read(f"probsT{t}0")
                    was_read(f"probsT{t}1")
                    pe.wait_ge(v_blocks_ready, 1)
                    w = 2 * (DK + 1)
                    for c in range(PAIRS):
                        mm = pe.matmul(ps[:, c * w:(c + 1) * w], probsT[:, t, c, :],
                                       v_blocks[:, c, :, :].rearrange("p a d -> p (a d)"), start=True, stop=True)
                    give(mm, f"attn{t}")

                def turn_attn():
                    ps = take("attnT")
                    for t in range(TILES):
                        mm = pe.transpose(ps[:, t * P:(t + 1) * P], attn[:, t, :], ident[:])
                    give(mm, "attnT")

                def project_out():
                    ps = take("proj")
                    was_read("attnT")
                    for t in range(TILES):
                        mm = pe.matmul(ps[:, t * D:(t + 1) * D], attnT[:, t, :], wT[:, 3, :], start=True, stop=True)
                    give(mm, "proj")

                def turn_norm():
                    ps = take("normT")
                    pe.wait_ge(xn_ready, 1)
                    for t in range(TILES):
                        mm = pe.transpose(ps[:, t * P:(t + 1) * P], xn[:, t, :], ident[:])
                    give(mm, "normT")

                def similarities(t):
                    ps = take(f"sims{t}")
                    was_read("normT")
                    give(pe.matmul(ps[:], xnT[:, t * P:(t + 1) * P], sim_w[:], start=True, stop=True), f"sims{t}")

                def turn_sims(t, s):
                    pe.wait_ge(sims_split[t], 1)
                    ps = take(f"simsT{t}{s}")
                    for k in range(4):
                        src = sims_hl[:, t, 4 * s + k, :, :].rearrange("p a b -> p (a b)").bitcast(F32)
                        mm = pe.transpose(ps[:, k * P:(k + 1) * P], src, ident[:])
                    give(mm, f"simsT{t}{s}")

                def was_kept(g):
                    if g % RH in ACT_HEADS:
                        pe.wait_ge(kept_by_act, count_items(ACT_HEADS, first, g))
                    else:
                        pe.wait_ge(kept_by_dve, count_items(DVE_HEADS, first, g))

                def pairs(g):
                    if user_before(g) >= first and (route or user_before(g) < 0):
                        was_kept(user_before(g))
                    if g % RH == 0:
                        t = g // RH % TILES
                        was_read(f"simsT{t}0")
                        was_read(f"simsT{t}1")
                    for s in range(2):
                        mm = pe.matmul(pair_ps[pair_buf(g)][:, s * HALF:(s + 1) * HALF],
                                       simsT[:, g // RH % TILES, g % RH, :], spread_r[:, s * HALF:(s + 1) * HALF],
                                       start=True, stop=False, skip_group_check=True)
                    mm.then_inc(pairs_ready, 1)

                def lower(g):
                    pe.wait_ge(below_ready, g + 1)
                    for s in range(2):
                        mm = pe.matmul(pair_ps[pair_buf(g)][:, s * HALF:(s + 1) * HALF], neg_ident[:],
                                       below[:, g % 2, s * HALF:(s + 1) * HALF],
                                       start=False, stop=True, skip_group_check=True)
                    mm.then_inc(lowered_for_act if g % RH in ACT_HEADS else lowered_for_dve, 1)

                def gather(t):
                    was_kept(-1 if t else RH - 1)
                    pe.wait_ge(kept_pooled, 1 if t else 1 + tail)
                    for s in range(2):
                        ps = take(f"kept{t}{s}")
                        for src in (kept_sum, kept_act):
                            for c in range(4):
                                mm = pe.matmul(ps[:, c * P:(c + 1) * P], src[:, t, s, c * P:(c + 1) * P], ident[:],
                                               is_transpose=True, start=(src is kept_sum and c == 0),
                                               stop=(src is kept_act), skip_group_check=True)
                        give(mm, f"kept{t}{s}")

                def mix(t):
                    ps = take(f"out{t}")
                    pe.wait_ge(gated, 1 if t else 1 + tail)
                    for c in range(CHUNKS):
                        mm = pe.matmul(ps[:, 0:D], gatedT[:, c, :], up_sb[:, c, :],
                                       start=(c == 0), stop=(c == CHUNKS - 1))
                    give(mm, f"out{t}")

                for g in range(ITEMS):
                    if route and g:
                        lower(g - 1)
                    wait_long = user_before(g + 1) >= g - 1
                    if (late if g == ITEMS - 1 else route) and not wait_long:
                        pairs(g + 1)
                    if route and g == 0:
                        turn_sims(1, 0)
                        turn_sims(1, 1)
                    if late and g == 1:
                        turn_attn()
                    if tail and g == 1:
                        gather(1)
                    if late and g == 2:
                        project_out()
                    if early and g == 2:
                        turn_inputs()
                    if tail and g == 2:
                        mix(1)
                    if early and g == 4:
                        project()
                    if route and g in (3, 4, 5):
                        for n in {3: (0,), 4: (1,), 5: (2, 3)}[g]:
                            hidden(n)
                    if late and g == 6:
                        turn_norm()
                    if early and g == 6:
                        score(0)
                    if late and g == 7:
                        similarities(0)
                        similarities(1)
                    if early and g == 8:
                        score(1)
                    if route and g == 9:
                        gather(0)
                    if early and g in (10, 12):
                        turn_probs((g - 10) // 2)
                    if late and g == 11:
                        turn_sims(0, 0)
                    if early and g in (12, 14):
                        attend_values((g - 12) // 2)
                    if late and g == 13:
                        turn_sims(0, 1)
                    if route and g == 13:
                        mix(0)
                    if route and wait_long:
                        pairs(g + 1)
                    if route and g == 0:
                        pe.sem_inc(sims_split[1], -1)
                    if early and g == 2:
                        pe.sem_inc(ctx_loaded, -32)
                        pe.sem_inc(y_ready, -1)
                    if late and g == 6:
                        pe.sem_inc(xn_ready, -1)
                    if early and g == 8:
                        pe.sem_inc(k_blocks_ready, -1)
                    if (tail or route) and g == 9:
                        pe.sem_inc(kept_pooled, -(tail + route))
                    if early and g == 12:
                        pe.sem_inc(shifted, -TILES)
                    if late and g == 13:
                        pe.sem_inc(sims_split[0], -1)
                    if (tail or route) and g == 13:
                        pe.sem_inc(gated, -(tail + route))
                    if early and g == 14:
                        pe.sem_inc(v_blocks_ready, -1)
                    for kept, kind, last_wait in ((kept_by_act, ACT_HEADS, ITEMS - 1), (kept_by_dve, DVE_HEADS, ITEMS - 2)):
                        if (tail or route) and g == last_wait:
                            n = count_items(kind, first, ITEMS - 3 if route else -1)
                            pe.wait_ge(kept, n)
                            pe.sem_inc(kept, -n)

                if route:
                    lower(ITEMS - 1)
                    pe.sem_inc(below_ready, -ITEMS)
                for b in range(2):
                    if used[b]:
                        pe.wait_ge(misc_read[b], used[b])
                        pe.sem_inc(misc_read[b], -used[b])

            iteration(False, False, False, True)
            iteration(False, False, True, True)
            iteration(False, True, True, True)
            with pe.Fori(2, BATCH - 1):
                iteration(True, True, True, True)
            iteration(True, True, True, False)
            iteration(True, True, False, False)
            iteration(True, False, False, False)

        @block.scalar
        def _(act):
            act.wait_ge(loaded, 16 * 18)
            nc.scalar.activation(spread_r[:], spread_f[:], ACT.Identity)
            nc.scalar.activation(neg_ident[:], ident[:], ACT.Identity, scale=-1.0)
            nc.scalar.activation(bk_scaled[:], bk[:], ACT.Identity, scale=float(DK) ** -0.5)
            targets = [wT[:]] + [wqT[:, 4 * n:4 * n + 4, :] for n in range(4)]
            targets += [keysT[:].rearrange("p g s k -> p (g s) k")]
            targets += [downT[:, 4 * n:4 * n + 4, :] for n in range(2)]
            for n, dst in enumerate(targets):
                act.wait_ge(setup_pe, n + 1)
                src = banks[n].rearrange("p (a b) -> p a b", a=4)
                if n >= 6:
                    nc.scalar.activation(dst, src, ACT.Copy, scale=nw[:, 0:1]).then_inc(setup_act, 1)
                else:
                    nc.scalar.activation(dst, src, ACT.Copy).then_inc(setup_act, 1)
            act.wait_ge(setup_pe, 9)
            nc.scalar.activation(sim_w[:], banks[0], ACT.Copy, scale=nw[:, 0:1]).then_inc(setup_act, 3)

            def iteration(tail, route, late, early):
                plan, _, read = misc_plan(tail, route, late, early)

                def take(name):
                    b, _, k, _ = plan[name]
                    act.wait_ge(misc_for[b, "act"], k + 1)
                    return misc_ps[b], misc_read[b]

                def find_below(g):
                    act.wait_ge(pairs_ready, g + 1)
                    nc.scalar.activation(below[:, g % 2, :], pair_ps[pair_buf(g)][:], ACT.Relu, scale=-STEEP,
                                         bias=steep_cut[:, g // RH, g % RH:g % RH + 1]).then_inc(below_ready, 1)

                def keep(g):
                    t, n = g // RH, ACT_HEADS.index(g % RH)
                    dst = kept_act[:, t] if n == 0 else kept_a[:, n - 1]
                    act.wait_ge(lowered_for_act, count_items(ACT_HEADS, 0, g))
                    nc.scalar.activation(dst.rearrange("p s e -> p (s e)"), pair_ps[pair_buf(g)][:],
                                         ACT.Relu).then_inc(kept_by_act, 1)
                    if n:
                        nc.scalar.copy(flag[:, 5 + n:6 + n], ident[:, 0:1]).then_inc(kept_for_pool, 1)

                def turn_sims(t, s):
                    ps, done = take(f"simsT{t}{s}")
                    nc.scalar.activation(simsT[:, t, 4 * s:4 * s + 4, :],
                                         ps[:].rearrange("p (a b) -> p a b", a=4), ACT.Identity).then_inc(done, 1)

                def exps(t):
                    for s in range(2):
                        ps, done = take(f"probsT{t}{s}")
                        nc.scalar.activation(probsT[:, t, 4 * s:4 * s + 4, :],
                                             ps[:].rearrange("p (a b) -> p a b", a=4), ACT.Exp).then_inc(done, 1)

                def copy_sims(t):
                    ps, done = take(f"sims{t}")
                    nc.scalar.activation(sims[:, t, :, :, :].rearrange("p h s k -> p (h s k)"), ps[:],
                                         ACT.Identity).then_inc(sims_for_topk[t], 1)
                    nc.scalar.activation(sims_hl[:, t, :, 0, :], ps[:].rearrange("p (h k) -> p h k", h=RH),
                                         ACT.Identity).then_inc(done, 1)
                    nc.scalar.copy(flag[:, 3 + t:4 + t], ident[:, 0:1]).then_inc(sims_to_split, 1)

                def copy_scores(t):
                    for s in range(2):
                        ps, done = take(f"scores{t}{s}")
                        nc.scalar.activation(
                            scores[:, t, 8 * s:8 * s + 8, :], ps[:].rearrange("p (h k) -> p h k", h=8),
                            ACT.Identity).then_inc(done, 1)
                    nc.scalar.copy(flag[:, 1 + t:2 + t], ident[:, 0:1]).then_inc(scores_ready, 1)

                def load_table(func):
                    nc.scalar.activation(flag[:, 0:1], ident[:, 0:1], func)

                def gelu(n):
                    ps, done = take(f"hidden{n}")
                    nc.scalar.activation(geluT[:, 2 * n:2 * n + 2, :], ps[:].rearrange("p (a b) -> p a b", a=2),
                                         ACT.Gelu).then_inc(done, 1)

                for g in range(ITEMS):
                    if route and g % RH == 0:
                        act.wait_ge(cut_ready[g // RH], 1)
                    if route:
                        find_below(g)
                        if g % RH == 0:
                            act.sem_inc(cut_ready[g // RH], -1)
                        if (g - 1) % RH in ACT_HEADS and g:
                            keep(g - 1)
                    if route and g == 0:
                        turn_sims(1, 0)
                        turn_sims(1, 1)
                    if late and g == 1:
                        ps, done = take("attnT")
                        nc.scalar.activation(attnT[:].rearrange("p t q -> p (t q)"), ps[:, 0:TILES * P],
                                             ACT.Identity).then_inc(done, 1)
                    if route and g == 1:
                        load_table(ACT.Gelu)
                    if early and g == 2:
                        ps, done = take("inputsT")
                        nc.scalar.activation(ctxT[:], ps[:, 0:P], ACT.Identity)
                        nc.scalar.activation(yT[:], ps[:, P:P + SEQ], ACT.Identity).then_inc(done, 1)
                    if early and g == 4:
                        ps, done = take("qkv")
                        nc.scalar.activation(kT[:], ps[:, SEQ:SEQ + CTX], ACT.Identity,
                                             scale=float(DK) ** -0.5, bias=bk_scaled[:, 0:1])
                        nc.scalar.activation(v_in[:], ps[:, SEQ + CTX:SEQ + CTX + D], ACT.Identity).then_inc(v_ready, 1)
                        nc.scalar.activation(qT[:], ps[:, 0:SEQ], ACT.Identity, bias=bq[:, 0:1]).then_inc(done, 1)
                    if route and g in (3, 4, 5):
                        for n in {3: (0,), 4: (1,), 5: (2, 3)}[g]:
                            gelu(n)
                    if route and g == 5:
                        nc.scalar.copy(flag[:, 5:6], ident[:, 0:1]).then_inc(gelu_ready, 1)
                    if late and g == 6:
                        ps, done = take("normT")
                        nc.scalar.activation(xnT[:], ps[:, 0:SEQ], ACT.Identity).then_inc(done, 1)
                    if early and g == 6:
                        copy_scores(0)
                    if late and g in (7, 8):
                        copy_sims(g - 7)
                    if early and g == 8:
                        copy_scores(1)
                    if early and g == 9:
                        load_table(ACT.Exp)
                    if early and g in (10, 12):
                        exps((g - 10) // 2)
                    if late and g == 11:
                        turn_sims(0, 0)
                    if late and g == 13:
                        turn_sims(0, 1)

                if route:
                    act.sem_inc(pairs_ready, -ITEMS)
                    act.sem_inc(lowered_for_act, -TILES * len(ACT_HEADS))
                for b in range(2):
                    if read.get((b, "act")):
                        act.sem_inc(misc_for[b, "act"], -read[b, "act"])

            iteration(False, False, False, True)
            iteration(False, False, True, True)
            iteration(False, True, True, True)
            with act.Fori(2, BATCH - 1):
                iteration(True, True, True, True)
            iteration(True, True, True, False)
            iteration(True, True, False, False)
            iteration(True, False, False, False)

        @block.gpsimd
        def _(pool):
            nc.gpsimd.memset(neg_half[:], -0.5)
            pool.wait_ge(loaded, 16 * 18)
            nc.gpsimd.tensor_copy(v_blocks[:, :, :, DK],
                                  pair_mask[:].unsqueeze(1).to_broadcast([P, PAIRS, 2]))
            pool.drain()

            def iteration(tail, route, late, early):
                steps = [0]

                def inverse_root(dst, tmp, var, scale, shift):
                    nc.gpsimd.tensor_scalar(tmp[:], var, scale, shift, ALU.mult, ALU.add).then_inc(pool_step, 1)
                    steps[0] += 1
                    pool.wait_ge(pool_step, steps[0])
                    nc.gpsimd.tensor_tensor(dst[:], tmp[:], neg_half[:], ALU.pow).then_inc(rstd_ready, 1)

                def pair_cands(t, q):
                    pool.wait_ge(halves_sorted, (q + 1 if t else q + 1 + 2 * route))
                    hs = slice(4 * q, 4 * q + 4)
                    at = 0
                    for i0, ni, nj in RECTS:
                        a = sorted16[:, t, hs, 0, i0:i0 + ni].unsqueeze(3).to_broadcast([P, 4, ni, nj])
                        b = sorted16[:, t, hs, 1, 0:nj].unsqueeze(2).to_broadcast([P, 4, ni, nj])
                        dst = cands[:, t, hs, at:at + ni * nj].rearrange("p h (i j) -> p h i j", i=ni)
                        last = nc.gpsimd.tensor_tensor(dst, a, b, ALU.add)
                        at += ni * nj
                    last.then_inc(cands_ready, 1)

                def blocks():
                    pool.wait_ge(v_ready, 1)
                    shape = [P, HEADS, CTX]
                    nc.gpsimd.tensor_tensor(k_blocks[:], kT[:].unsqueeze(1).to_broadcast(shape),
                                            mask[:].unsqueeze(2).to_broadcast(shape), ALU.mult).then_inc(k_blocks_ready, 1)
                    nc.gpsimd.tensor_tensor(v_biased[:], v_in[:], bv[:], ALU.add).then_inc(pool_step, 1)
                    steps[0] += 1
                    pool.wait_ge(pool_step, steps[0])
                    nc.gpsimd.tensor_tensor(v_blocks[:, :, :, 0:DK],
                                            v_biased[:].rearrange("p (c a d) -> p c a d", a=2, d=DK),
                                            pair_mask[:].unsqueeze(1).unsqueeze(3).to_broadcast([P, PAIRS, 2, DK]),
                                            ALU.mult).then_inc(v_blocks_ready, 1)
                    nc.gpsimd.memset(pool_mark[:], 0.0).then_inc(inputs_read, 1)

                def shift_scores(t):
                    pool.wait_ge(peak_ready, t + 1)
                    nc.gpsimd.tensor_tensor(scores[:, t], scores[:, t],
                                            peak[:, t, :].unsqueeze(2).to_broadcast([P, HEADS, CTX]),
                                            ALU.subtract).then_inc(shifted, 1)

                def split(t):
                    pool.wait_ge(sims_to_split, t + 1)
                    nc.gpsimd.tensor_tensor(
                        sims_hl[:, t, :, 1, :], sims[:, t, :, :, :].rearrange("p h s k -> p h (s k)"),
                        sims_hl[:, t, :, 0, :].bitcast(F32), ALU.subtract).then_inc(sims_split[t], 1)

                def add_act(t, n):
                    pool.wait_ge(kept_for_pool, 2 * t + n + 1)
                    if n == 1:
                        pool.wait_ge(pool_step, added[t])
                    ins = nc.gpsimd.tensor_tensor(kept_act[:, t], kept_act[:, t], kept_a[:, n], ALU.add)
                    if n == 0:
                        ins.then_inc(pool_step, 1)
                        steps[0] += 1
                        added[t] = steps[0]
                    else:
                        ins.then_inc(kept_pooled, 1)

                added = {}
                if early:
                    pool.wait_ge(var_ready, 1)
                    inverse_root(rstd, shifted_var, mean_var[:, :, 1], 1.0, EPS)
                if late:
                    pool.wait_ge(var_ready, 1 + early)
                    inverse_root(rstd2, shifted_var2, mean_var2[:, :, 1], 1.0 + EPS, EPS * EPS)
                if early:
                    for t in range(TILES):
                        nc.gpsimd.tensor_tensor(x_bias[:, t, :], x_in[:, t, :], bo[:], ALU.add)
                if route:
                    pair_cands(1, 0)
                if early:
                    blocks()
                if route:
                    pair_cands(1, 1)
                    add_act(0, 0)
                if early:
                    shift_scores(0)
                if route:
                    add_act(0, 1)
                if late:
                    split(0)
                if early:
                    shift_scores(1)
                if late:
                    split(1)
                if late:
                    pair_cands(0, 0)
                    pair_cands(0, 1)
                if route:
                    add_act(1, 0)
                    add_act(1, 1)

                if early:
                    pool.sem_inc(v_ready, -1)
                    pool.sem_inc(peak_ready, -TILES)
                if late:
                    pool.sem_inc(sims_to_split, -TILES)
                if late or early:
                    pool.sem_inc(var_ready, -(late + early))
                if steps[0]:
                    pool.wait_ge(pool_step, steps[0])
                    pool.sem_inc(pool_step, -steps[0])
                if route:
                    pool.sem_inc(kept_for_pool, -2 * TILES)
                if route or late:
                    pool.sem_inc(halves_sorted, -2 * (route + late))

            iteration(False, False, False, True)
            iteration(False, False, True, True)
            iteration(False, True, True, True)
            with pool.Fori(2, BATCH - 1):
                iteration(True, True, True, True)
            iteration(True, True, True, False)
            iteration(True, True, False, False)
            iteration(True, False, False, False)

        @block.vector
        def _(dve):
            dve.wait_ge(loaded, 16 * 18)

            def iteration(tail, route, late, early):
                plan, _, read = misc_plan(tail, route, late, early)
                steps = [0]

                def step(ins):
                    ins.then_inc(dve_step, 1)
                    steps[0] += 1
                    return steps[0]

                def take(name):
                    b, _, k, _ = plan[name]
                    dve.wait_ge(misc_for[b, "dve"], k + 1)
                    return misc_ps[b], misc_read[b]

                def variance(src, st, mv):
                    for t in range(TILES):
                        n = step(nc.vector.bn_stats(st[:, t, :], src[:, t, :]))
                    dve.wait_ge(dve_step, n)
                    nc.vector.bn_aggr(mv[:, 0, :], st[:, 0, :])
                    nc.vector.bn_aggr(mv[:, 1, :], st[:, 1, :]).then_inc(var_ready, 1)

                def normalise(dst, src, mv, r, ready):
                    for t in range(TILES):
                        last = nc.vector.tensor_scalar(dst[:, t, :], src[:, t, :], mv[:, t, 0:1], r[:, t:t + 1],
                                                       ALU.subtract, ALU.mult)
                    last.then_inc(ready, 1)

                reached = {}
                summed = [0]

                def lists(q):
                    return [(h, s) for h in range(4 * q, 4 * q + 4) for s in range(2)]

                def sort_first(t, q):
                    for h, s in lists(q):
                        reached[t, h, s] = step(nc.vector.max(sorted16[:, t, h, s, 0:8], sims[:, t, h, s, :]))

                def sort_rest(t, q):
                    for h, s in lists(q):
                        dve.wait_ge(dve_step, reached[t, h, s])
                        reached[t, h, s] = step(nc.vector.match_replace(
                            rest[:, t, h, s, :], sorted16[:, t, h, s, 0:8], sims[:, t, h, s, :], LOWEST))

                def sort_second(t, q):
                    for h, s in lists(q):
                        dve.wait_ge(dve_step, reached[t, h, s])
                        last = nc.vector.max(sorted16[:, t, h, s, 8:16], rest[:, t, h, s, :])
                    last.then_inc(halves_sorted, 1)

                def best_first(t, q):
                    dve.wait_ge(cands_ready, q + 1 if t else q + 1 + 2 * route)
                    for h in range(4 * q, 4 * q + 4):
                        reached[t, h] = step(nc.vector.max(best[:, t, h, 0:8], cands[:, t, h, :]))

                def best_rest(t, q):
                    for h in range(4 * q, 4 * q + 4):
                        dve.wait_ge(dve_step, reached[t, h])
                        reached[t, h] = step(nc.vector.match_replace(
                            cands_rest[:, t, h, :], best[:, t, h, 0:8], cands[:, t, h, :], LOWEST))

                def best_second(t, q):
                    for h in range(4 * q, 4 * q + 4):
                        dve.wait_ge(dve_step, reached[t, h])
                        reached[t, h] = step(nc.vector.max(best[:, t, h, 8:16], cands_rest[:, t, h, :]))

                def set_cut(t):
                    m = step(nc.vector.tensor_tensor(top_sim[:, t, :], sorted16[:, t, :, 0, 0], sorted16[:, t, :, 1, 0],
                                                     ALU.max))
                    dve.wait_ge(dve_step, max(m, reached[t, RH - 1]))
                    n = step(nc.vector.scalar_tensor_tensor(cut_raw[:, t, :], top_sim[:, t, :], -MARGIN,
                                                            best[:, t, :, TOP - 1], ALU.mult, ALU.add))
                    dve.wait_ge(dve_step, n)
                    n = step(nc.vector.tensor_scalar(cut[:, t, :], cut_raw[:, t, :], TINY, None, ALU.max))
                    dve.wait_ge(dve_step, n)
                    nc.vector.tensor_scalar(steep_cut[:, t, :], cut[:, t, :], STEEP, None, ALU.mult)\
                        .then_inc(cut_ready[t], 1)

                def find_peak(t):
                    dve.wait_ge(scores_ready, t + 1)
                    nc.vector.tensor_reduce(peak[:, t, :], scores[:, t], AX.X, ALU.max).then_inc(peak_ready, 1)

                search = (
                    {8: [(sort_first, 0), (sort_rest, 0)], 9: [(sort_second, 0)], 10: [(sort_first, 1)],
                     11: [(sort_rest, 1)], 12: [(sort_second, 1), (best_first, 0)],
                     13: [(best_rest, 0), (best_second, 0), (best_first, 1)], 14: [(best_rest, 1), (best_second, 1)]},
                    {0: [(sort_first, 0)], 2: [(sort_rest, 0)], 3: [(sort_second, 0)], 4: [(sort_first, 1)],
                     5: [(sort_rest, 1), (sort_second, 1), (best_first, 0)],
                     6: [(best_rest, 0), (best_second, 0), (best_first, 1)], 7: [(best_rest, 1), (best_second, 1)]},
                )

                def threshold(t, g):
                    for step_of_search, q in search[t].get(g, []):
                        step_of_search(t, q)
                    if g == max(search[t]):
                        set_cut(t)

                def add_kept(g):
                    t, h = g // RH, g % RH
                    dve.wait_ge(lowered_for_dve, count_items(DVE_HEADS, 0, g))
                    if h - 1 in DVE_HEADS:
                        dve.wait_ge(dve_step, summed[0])
                    total = kept_sum[:, t].rearrange("p s e -> p (s e)")
                    ps = pair_ps[pair_buf(g)][:]
                    if h == DVE_HEADS[0]:
                        ins = nc.vector.tensor_scalar(total, ps, 0.0, None, ALU.max)
                    else:
                        ins = nc.vector.scalar_tensor_tensor(total, ps, 0.0, total, ALU.max, ALU.add)
                    ins.then_inc(kept_by_dve, 1)
                    if h + 1 in DVE_HEADS:
                        summed[0] = step(nc.vector.memset(mark[:, 2:3], 0.0))

                def divide(t):
                    ps, done = take(f"attn{t}")
                    v = ps[:, 0:HEADS * (DK + 1)].rearrange("p (h d) -> p h d", d=DK + 1)
                    n = step(nc.vector.reciprocal(rsum[:, t, :], v[:, :, DK]))
                    dve.wait_ge(dve_step, n)
                    nc.vector.tensor_tensor(attn[:, t, :].rearrange("p (h d) -> p h d", d=DK), v[:, :, 0:DK],
                                            rsum[:, t, :].unsqueeze(2).to_broadcast([P, HEADS, DK]),
                                            ALU.mult).then_inc(done, 1)

                def residual():
                    ps, done = take("proj")
                    n = step(nc.vector.tensor_tensor(x1_new[:, 0, :], ps[:, 0:D], x_bias[:, 0, :], ALU.add))
                    nc.vector.tensor_tensor(x1_new[:, 1, :], ps[:, D:2 * D], x_bias[:, 1, :], ALU.add).then_inc(done, 1)
                    dve.wait_ge(dve_step, n)
                    n = step(nc.vector.bn_stats(stats2[:, 0, :], x1_new[:, 0, :]))
                    dve.wait_ge(dve_step, n)
                    n = step(nc.vector.bn_stats(stats2[:, 1, :], x1_new[:, 1, :]))
                    dve.wait_ge(dve_step, n)
                    nc.vector.bn_aggr(mean_var2[:, 0, :], stats2[:, 0, :])
                    nc.vector.bn_aggr(mean_var2[:, 1, :], stats2[:, 1, :]).then_inc(var_ready, 1)

                def gate(t):
                    if t == 0:
                        dve.wait_ge(gelu_ready, 1)
                    for s in range(2):
                        ps, done = take(f"kept{t}{s}")
                        nc.vector.tensor_tensor(gatedT[:, 4 * s:4 * s + 4, :], ps[:].rearrange("p (c t) -> p c t", c=4),
                                                geluT[:, 4 * s:4 * s + 4, t * P:(t + 1) * P], ALU.mult)\
                            .then_inc(done, 1)
                    nc.vector.memset(mark[:, 3:4], 0.0).then_inc(gated, 1)

                def finish(t):
                    if t == 0 and tail:
                        dve.wait_ge(out_free, 1)
                    ps, done = take(f"out{t}")
                    nc.vector.tensor_tensor(y_out[:, t, :], ps[:, 0:D], x1_tail[:] if t else x1[:, 0, :],
                                            ALU.add).then_inc(done, 1)
                    nc.vector.memset(mark[:, t:t + 1], 0.0).then_inc(out_ready, 1)

                for g in range(ITEMS):
                    if route and g and (g - 1) % RH in DVE_HEADS:
                        add_kept(g - 1)
                    if early and g == 0:
                        dve.wait_ge(x_loaded, 16)
                        variance(x_in, stats, mean_var)
                    if tail and g == 0:
                        n = step(nc.vector.tensor_copy(x1_tail[:], x1[:, 1, :]))
                        dve.wait_ge(dve_step, n)
                    if route and g == 0:
                        nc.vector.tensor_copy(x1[:], x1_new[:])
                    if tail and g == 1:
                        gate(1)
                    if late and g == 2:
                        residual()
                    if early and g == 1:
                        dve.wait_ge(rstd_ready, 1)
                        normalise(y, x_in, mean_var, rstd, y_ready)
                    if route and g < RH:
                        if g == 0:
                            dve.wait_ge(sims_for_topk[1], 1)
                        threshold(1, g)
                        if g == 0:
                            dve.sem_inc(sims_for_topk[1], -1)
                    if late and g >= RH:
                        if g == RH:
                            dve.wait_ge(sims_for_topk[0], 1)
                        threshold(0, g)
                        if g == RH:
                            dve.sem_inc(sims_for_topk[0], -1)
                    if route and g == 9:
                        gate(0)
                        dve.sem_inc(gelu_ready, -1)
                    if early and g == 9:
                        find_peak(1)
                        dve.sem_inc(scores_ready, -TILES)
                    if late and g == 4:
                        dve.wait_ge(rstd_ready, 1 + early)
                        normalise(xn, x1_new, mean_var2, rstd2, xn_ready)
                    if tail and g == 2:
                        finish(1)
                    if early and g == 7:
                        find_peak(0)
                    if early and g == 13:
                        divide(0)
                    if route and g == 13:
                        finish(0)
                    if early and g == 15:
                        divide(1)
                    if early and g == 0:
                        dve.sem_inc(x_loaded, -16)
                    if (late or early) and g == 4:
                        dve.sem_inc(rstd_ready, -(late + early))
                    if (route or late) and g == 14:
                        dve.sem_inc(cands_ready, -2 * (route + late))
                    if tail and route and g == 14:
                        dve.sem_inc(out_free, -1)

                if route:
                    add_kept(ITEMS - 1)
                    dve.sem_inc(lowered_for_dve, -TILES * len(DVE_HEADS))
                for b in range(2):
                    if read.get((b, "dve")):
                        dve.sem_inc(misc_for[b, "dve"], -read[b, "dve"])
                if steps[0]:
                    dve.wait_ge(dve_step, steps[0])
                    dve.sem_inc(dve_step, -steps[0])

            iteration(False, False, False, True)
            iteration(False, False, True, True)
            iteration(False, True, True, True)
            with dve.Fori(2, BATCH - 1):
                iteration(True, True, True, True)
            iteration(True, True, True, False)
            iteration(True, True, False, False)
            iteration(True, False, False, False)


_INS = [("x", "x"), ("ctx_1024", "ctx"), ("L0_xattn_W_Q", "W_Q"), ("L0_xattn_b_Q", "b_Q"), ("L0_xattn_W_K", "W_K"),
        ("L0_xattn_b_K", "b_K"), ("L0_xattn_W_V", "W_V"), ("L0_xattn_b_V", "b_V"), ("L0_xattn_W_O", "W_O"),
        ("L0_xattn_b_O", "b_O"), ("L0_ffn_norm_w", "norm_w"), ("L0_ffn_wq", "wq"), ("L0_ffn_keys", "keys"),
        ("L0_ffn_expert_down", "down"), ("L0_ffn_expert_up", "up")]


def kernel(**inputs):
    import numpy as np
    import concourse.bacc as bacc
    from concourse import mybir as mb
    from concourse.bass_utils import run_bass_kernel_spmd

    arrays = {f"in_{short}": np.ascontiguousarray(inputs[name]) for name, short in _INS}
    arrays["in_eye"] = np.eye(P, dtype=np.float32)
    row, col = np.arange(P)[:, None] % (2 * NK), np.arange(EXPERTS)[None, :]
    arrays["in_spread"] = ((row == col // NK) | (row == NK + col % NK)).astype(np.float32)
    arrays["in_head_mask"] = (np.arange(P)[:, None] // DK == np.arange(HEADS)[None, :]).astype(np.float32)
    arrays["in_key_mask"] = (np.arange(P)[:, None] // CTX == np.arange(2)[None, :]).astype(np.float32)

    nc = bacc.Bacc("TRN2", target_bir_lowering=False, num_devices=1)
    aps = [nc.dram_tensor(n, a.shape, mb.dt.from_np(a.dtype), kind="ExternalInput").ap() for n, a in arrays.items()]
    out = nc.dram_tensor("out", (BATCH, SEQ, D), mb.dt.float32, kind="ExternalOutput").ap()
    xattn_peer_kernel(nc, *aps, out)
    r = run_bass_kernel_spmd(nc, [arrays], core_ids=[0])
    return r.results[0]["out"]
```

```python
from contextlib import ExitStack

import concourse.bass as bass
from concourse import mybir

ALU = mybir.AluOpType
ACT = mybir.ActivationFunctionType
AX = mybir.AxisListType
F32 = mybir.dt.float32
F32R = mybir.dt.float32r
BF16 = mybir.dt.bfloat16

P = 128
D = 128
BATCH, SEQ, CTX = 16, 256, 64
TILES = SEQ // P
HEADS, DK = 16, 8
PAIRS = HEADS // 2
EPS = 1e-5
RH, NK, TOP = 8, 32, 16
EXPERTS = NK * NK
CHUNKS = EXPERTS // P
HALF = 512
LOWEST = -3.0e38
TINY = 1e-37
STEEP = float(2 ** 30)
MARGIN = float(2 ** -20)

RECTS = [(0, 1, 16), (1, 1, 8), (2, 2, 5), (4, 4, 3), (8, 8, 1)]
CANDS = sum(n * m for _, n, m in RECTS)

ITEMS = TILES * RH
ACT_ITEMS = (1, 2, 5, 10, 12, 14)
DVE_ITEMS = tuple(g for g in range(ITEMS) if g not in ACT_ITEMS)
TILE_ACT_ITEMS = [[g for g in ACT_ITEMS if g // RH == t] for t in range(TILES)]
assert all(len(items) == 3 and (t + 1) * RH - 1 not in items for t, items in enumerate(TILE_ACT_ITEMS))
SHORT = 8
ROUND = [g % 3 for g in range(ITEMS - 1)] + [1]
PAIR_BUF = [ROUND[(g - 1 - SHORT) % ITEMS] for g in range(ITEMS)]


def pair_buf(g):
    return PAIR_BUF[g % ITEMS]


def user_before(g):
    n = g - 1
    while pair_buf(n) != pair_buf(g):
        n -= 1
    return n


def count_items(kind, first, last):
    return sum(g % ITEMS in kind for g in range(first, last + 1))


SHARED = [
    (0, "route", "simsT10", "act"), (0, "route", "simsT11", "act"),
    (1, "late", "attnT", "act"), (1, "tail", "kept10", "dve"), (1, "tail", "kept11", "dve"),
    (2, "late", "proj", "dve"), (2, "early", "inputsT", "act"),
    (3, "route", "hidden0", "act"), (3, "tail", "out1", "dve"),
    (4, "early", "qkv", "act"), (4, "route", "hidden1", "act"),
    (5, "route", "hidden2", "act"), (5, "route", "hidden3", "act"),
    (6, "late", "normT", "act"), (6, "early", "scores00", "act"), (6, "early", "scores01", "act"),
    (7, "late", "sims0", "act"), (7, "late", "sims1", "act"),
    (8, "early", "scores10", "act"), (8, "early", "scores11", "act"),
    (9, "route", "kept00", "dve"), (9, "route", "kept01", "dve"),
    (10, "early", "probsT00", "act"), (10, "early", "probsT01", "act"),
    (11, "late", "simsT00", "act"),
    (12, "early", "probsT10", "act"), (12, "early", "probsT11", "act"), (12, "early", "attn0", "dve"),
    (13, "late", "simsT01", "act"), (13, "route", "out0", "dve"),
    (14, "early", "attn1", "dve"),
]


def misc_plan(tail, route, late, early):
    on = {"tail": tail, "route": route, "late": late, "early": early}
    order = [(name, reader) for _, stage, name, reader in SHARED if on[stage]]
    plan, used, read = {}, [0, 0], {}
    for n, (name, reader) in enumerate(order):
        b = n % 2
        k = read.get((b, reader), 0)
        plan[name] = (b, used[b], k, reader)
        used[b] += 1
        read[(b, reader)] = k + 1
    return plan, used, read


def xattn_peer_kernel(nc, x, ctx, W_Q, b_Q, W_K, b_K, W_V, b_V, W_O, b_O,
                      norm_w, wq, keys, down, up, eye, spread, head_mask, key_mask, out):
    with ExitStack() as stack:
        def sb(name, shape, dt=F32):
            return stack.enter_context(nc.sbuf_tensor(name, shape, dt))

        def sem(name):
            return stack.enter_context(nc.semaphore(name))

        ident = sb("ident", [P, P])
        neg_ident = sb("neg_ident", [P, P], BF16)
        spread_f = sb("spread_f", [P, EXPERTS])
        spread_r = sb("spread_r", [P, EXPERTS], F32R)
        mask = sb("mask", [P, HEADS])
        pair_mask = sb("pair_mask", [P, 2])
        pool_mark = sb("pool_mark", [P, 1])
        v_biased = sb("v_biased", [P, D])
        w_nat = sb("w_nat", [P, 4, D])
        wT = sb("wT", [P, 4, D])
        bq = sb("bq", [P, 1])
        bk = sb("bk", [P, 1])
        bk_scaled = sb("bk_scaled", [P, 1])
        bv = sb("bv", [P, D])
        bo = sb("bo", [P, D])
        nw = sb("nw", [P, 1])
        wq_nat = sb("wq_nat", [P, 2 * RH, P])
        wqT = sb("wqT", [P, 2 * RH, P])
        keys_nat = sb("keys_nat", [P, 2, 2, P])
        keysT = sb("keysT", [P, 2, 2, P])
        sim_w = sb("sim_w", [P, RH * 2 * NK])
        down_nat = sb("down_nat", [P, CHUNKS, D])
        downT = sb("downT", [P, CHUNKS, P])
        up_sb = sb("up_sb", [P, CHUNKS, D])
        neg_half = sb("neg_half", [P, TILES])

        x_in = sb("x_in", [P, TILES, D])
        ctx_in = sb("ctx_in", [P, D])
        x_bias = sb("x_bias", [P, TILES, D])
        stats = sb("stats", [P, TILES, 6])
        mean_var = sb("mean_var", [P, TILES, 2])
        stats2 = sb("stats2", [P, TILES, 6])
        mean_var2 = sb("mean_var2", [P, TILES, 2])
        shifted_var = sb("shifted_var", [P, TILES])
        rstd = sb("rstd", [P, TILES])
        shifted_var2 = sb("shifted_var2", [P, TILES])
        rstd2 = sb("rstd2", [P, TILES])
        y = sb("y", [P, TILES, D])
        yT = sb("yT", [P, SEQ])
        ctxT = sb("ctxT", [P, P])
        qT = sb("qT", [P, SEQ])
        kT = sb("kT", [P, CTX])
        v_in = sb("v_in", [P, D])
        k_blocks = sb("k_blocks", [P, HEADS, CTX])
        v_blocks = sb("v_blocks", [P, PAIRS, 2, DK + 1])
        scores = sb("scores", [P, TILES, HEADS, CTX])
        peak = sb("peak", [P, TILES, HEADS])
        probsT = sb("probsT", [P, TILES, PAIRS, P])
        rsum = sb("rsum", [P, TILES, HEADS])
        attn = sb("attn", [P, TILES, D])
        attnT = sb("attnT", [P, TILES, P])
        x1_new = sb("x1_new", [P, TILES, D])
        x1 = sb("x1", [P, TILES, D])
        x1_tail = sb("x1_tail", [P, D])
        xn = sb("xn", [P, TILES, D])
        xnT = sb("xnT", [P, SEQ])
        flag = sb("flag", [P, 16])

        sims = sb("sims", [P, TILES, RH, 2, NK])
        sims_hl = sb("sims_hl", [P, TILES, RH, 2, 2 * NK], F32R)
        simsT = sb("simsT", [P, TILES, RH, P], F32R)
        sorted16 = sb("sorted16", [P, TILES, RH, 2, TOP])
        rest = sb("rest", [P, TILES, RH, 2, NK])
        cands = sb("cands", [P, TILES, RH, CANDS])
        cands_rest = sb("cands_rest", [P, TILES, RH, CANDS])
        best = sb("best", [P, TILES, RH, TOP])
        top_sim = sb("top_sim", [P, TILES, RH])
        cut_raw = sb("cut_raw", [P, TILES, RH])
        cut = sb("cut", [P, TILES, RH])
        steep_cut = sb("steep_cut", [P, TILES, RH])
        kept_sum = sb("kept_sum", [P, TILES, 2, HALF])
        kept_act = sb("kept_act", [P, TILES, 2, HALF])
        kept_a = sb("kept_a", [P, 2, 2, HALF])
        below = sb("below", [P, 2, 2 * HALF], BF16)
        geluT = sb("geluT", [P, CHUNKS, SEQ])
        gatedT = sb("gatedT", [P, CHUNKS, P])
        y_out = sb("y_out", [P, TILES, D])
        mark = sb("mark", [P, 8])

        pair_ps = [stack.enter_context(nc.psum_tensor(f"pair_ps{n}", [P, 2 * HALF], F32)) for n in range(3)]
        misc_ps = [stack.enter_context(nc.psum_tensor(f"misc_ps{n}", [P, HALF], F32)) for n in range(2)]
        banks = [ps[:, s * HALF:(s + 1) * HALF] for ps in pair_ps for s in range(2)] + [ps[:] for ps in misc_ps]

        attention_loaded = sem("attention_loaded")
        blocks_loaded = sem("blocks_loaded")
        expert_loaded = sem("expert_loaded")
        others_loaded = sem("others_loaded")
        setup_pe = sem("setup_pe")
        setup_act = sem("setup_act")
        x_loaded = sem("x_loaded")
        ctx_loaded = sem("ctx_loaded")
        inputs_read = sem("inputs_read")
        var_ready = sem("var_ready")
        rstd_ready = sem("rstd_ready")
        y_ready = sem("y_ready")
        v_ready = sem("v_ready")
        k_blocks_ready = sem("k_blocks_ready")
        v_blocks_ready = sem("v_blocks_ready")
        scores_ready = sem("scores_ready")
        peak_ready = sem("peak_ready")
        shifted = sem("shifted")
        xn_ready = sem("xn_ready")
        sims_for_topk = [sem(f"sims{t}_for_topk") for t in range(TILES)]
        sims_to_split = sem("sims_to_split")
        sims_split = [sem(f"sims{t}_split") for t in range(TILES)]
        halves_sorted = sem("halves_sorted")
        cands_ready = sem("cands_ready")
        cut_ready = [sem(f"cut{t}_ready") for t in range(TILES)]
        pairs_ready = sem("pairs_ready")
        below_ready = sem("below_ready")
        lowered_for_act = sem("lowered_for_act")
        lowered_for_dve = sem("lowered_for_dve")
        kept_by_act = sem("kept_by_act")
        kept_by_dve = sem("kept_by_dve")
        kept_for_pool = sem("kept_for_pool")
        kept_pooled = sem("kept_pooled")
        gelu_ready = sem("gelu_ready")
        gated = sem("gated")
        out_ready = sem("out_ready")
        out_stored = sem("out_stored")
        out_free = sem("out_free")
        misc_for = {(b, e): sem(f"misc{b}_for_{e}") for b in range(2) for e in ("act", "dve")}
        misc_read = [sem(f"misc{b}_read") for b in range(2)]
        act_step = sem("act_step")
        dve_step = sem("dve_step")
        pool_step = sem("pool_step")

        x_v = x.rearrange("b (t p) d -> b p t d", p=P)
        out_v = out.rearrange("b (t p) d -> b p t d", p=P)

        block = stack.enter_context(nc.Block())

        @block.sync
        def _(sp):
            def row(vector):
                return vector.rearrange("(o d) -> o d", o=1).to_broadcast([P, D])

            def column(vector):
                return vector.rearrange("(p o) -> p o", o=1)

            attention_loads = [
                (ident[:], eye), (w_nat[:, 0, :], W_Q), (w_nat[:, 1, :], W_K), (w_nat[:, 2, :], W_V),
                (w_nat[:, 3, :], W_O), (bq[:], column(b_Q)), (bk[:], column(b_K)),
            ]
            attention_late_loads = [(bv[:], row(b_V)), (bo[:], row(b_O)), (mask[:], head_mask), (pair_mask[:], key_mask)]
            expert_loads = [(wq_nat[:].rearrange("p c d -> p (c d)"), wq)]
            expert_loads += [(keys_nat[:, g, :, :], keys[4 * g:4 * g + 4].rearrange("h k s d -> (h k) s d"))
                             for g in range(2)]
            expert_loads += [(down_nat[:], down.rearrange("(c p) d -> p c d", p=P)), (nw[:], column(norm_w))]
            other_loads = [(spread_f[:], spread), (up_sb[:], up.rearrange("(c p) d -> p c d", p=P))]
            assert [len(loads) for loads in (attention_loads, attention_late_loads, expert_loads, other_loads)] == [7, 4, 5, 2]

            def load_tokens(b):
                sp.dma_start(x_in[:], x_v[b]).then_inc(x_loaded, 16)

            def load_context(b):
                sp.dma_start(ctx_in[0:CTX, :], ctx[b]).then_inc(ctx_loaded, 16)
                sp.dma_start(ctx_in[CTX:P, :], ctx[b]).then_inc(ctx_loaded, 16)

            def store_batch(b):
                for t in range(TILES):
                    sp.wait_ge(out_ready, t + 1)
                    sp.dma_start(out_v[b, :, t, :], y_out[:, t, :]).then_inc(out_stored, 16)
                sp.sem_inc(out_ready, -TILES)
                sp.wait_ge(out_stored, 16 * TILES)
                sp.sem_inc(out_stored, -16 * TILES)
                sp.sem_inc(out_free, 1)

            def next_batch(b):
                sp.wait_ge(inputs_read, 1)
                sp.sem_inc(inputs_read, -1)
                load_tokens(b)
                load_context(b)

            load_tokens(0)
            for dst, src in attention_loads:
                sp.dma_start(dst, src).then_inc(attention_loaded, 16)
            load_context(0)
            for dst, src in attention_late_loads:
                sp.dma_start(dst, src).then_inc(blocks_loaded, 16)
            for dst, src in expert_loads:
                sp.dma_start(dst, src).then_inc(expert_loaded, 16)
            for dst, src in other_loads:
                sp.dma_start(dst, src).then_inc(others_loaded, 16)
            next_batch(1)
            next_batch(2)
            with sp.Fori(1, BATCH - 2) as i:
                next_batch(i + 2)
                store_batch(i - 1)
            for b in range(BATCH - 3, BATCH):
                store_batch(b)

        @block.tensor
        def _(pe):
            pe.wait_ge(attention_loaded, 16 * 7)

            def turn_weights(n, sources):
                for k, src in enumerate(sources):
                    mm = pe.transpose(banks[n][:, k * P:(k + 1) * P], src, ident[:])
                mm.then_inc(setup_pe, 1)

            def setup_step(g):
                if g == 6:
                    pe.wait_ge(expert_loaded, 16 * 5)
                    turn_weights(0, [wq_nat[:, n, :] for n in range(4)])
                    turn_weights(1, [wq_nat[:, n, :] for n in range(4, 8)])
                if g == 8:
                    turn_weights(2, [wq_nat[:, n, :] for n in range(8, 12)])
                    turn_weights(3, [wq_nat[:, n, :] for n in range(12, 16)])
                    turn_weights(4, [keys_nat[:, n, s, :] for n in range(2) for s in range(2)])
                if g == 9:
                    turn_weights(5, [down_nat[:, c, :] for c in range(4)])
                if g == 11:
                    pe.wait_ge(setup_act, 6)
                    turn_weights(1, [down_nat[:, c, :] for c in range(4, 8)])
                if g == 13:
                    for h in range(RH):
                        for s in range(2):
                            at = (2 * h + s) * NK
                            mm = pe.matmul(banks[0][:, at:at + NK], wqT[:, 2 * h + s, :],
                                           keysT[:, h // 4, s, (h % 4) * NK:(h % 4 + 1) * NK], start=True, stop=True)
                    mm.then_inc(setup_pe, 1)
                if g == ITEMS - 1:
                    pe.wait_ge(setup_act, 9)
                    pe.wait_ge(others_loaded, 16 * 2)

            turn_weights(6, [w_nat[:, n, :] for n in range(4)])
            pe.wait_ge(setup_act, 1)

            def iteration(tail, route, late, early, begin=False):
                plan, used, _ = misc_plan(tail, route, late, early)
                first = -2 if tail else 0

                def take(name):
                    b, before, _, _ = plan[name]
                    if before:
                        pe.wait_ge(misc_read[b], before)
                    return misc_ps[b]

                def give(mm, name):
                    b, _, _, reader = plan[name]
                    mm.then_inc(misc_for[b, reader], 1)

                def was_read(name):
                    b, before, _, _ = plan[name]
                    pe.wait_ge(misc_read[b], before + 1)

                def hidden(n):
                    ps = take(f"hidden{n}")
                    for c in (2 * n, 2 * n + 1):
                        mm = pe.matmul(ps[:, (c % 2) * SEQ:(c % 2 + 1) * SEQ], downT[:, c, :], xnT[:],
                                       start=True, stop=True)
                    give(mm, f"hidden{n}")

                def turn_inputs():
                    ps = take("inputsT")
                    pe.wait_ge(ctx_loaded, 32)
                    pe.transpose(ps[:, 0:P], ctx_in[:], ident[:])
                    pe.wait_ge(y_ready, 1)
                    for t in range(TILES):
                        mm = pe.transpose(ps[:, (t + 1) * P:(t + 2) * P], y[:, t, :], ident[:])
                    give(mm, "inputsT")

                def project():
                    ps = take("qkv")
                    was_read("inputsT")
                    pe.matmul(ps[:, SEQ:SEQ + CTX], wT[:, 1, :], ctxT[:, 0:CTX], start=True, stop=True)
                    pe.matmul(ps[:, SEQ + CTX:SEQ + CTX + D], ctxT[:], wT[:, 2, :], start=True, stop=True)
                    give(pe.matmul(ps[:, 0:SEQ], wT[:, 0, :], yT[:], start=True, stop=True), "qkv")

                def score(t):
                    was_read("qkv")
                    pe.wait_ge(k_blocks_ready, 1)
                    for s in range(2):
                        ps = take(f"scores{t}{s}")
                        give(pe.matmul(ps[:], qT[:, t * P:(t + 1) * P],
                                       k_blocks[:, s * 8:(s + 1) * 8, :].rearrange("p h k -> p (h k)"),
                                       start=True, stop=True), f"scores{t}{s}")

                def turn_probs(t):
                    pe.wait_ge(shifted, t + 1)
                    flat = scores[:, t, :, :].rearrange("p h k -> p (h k)")
                    for s in range(2):
                        ps = take(f"probsT{t}{s}")
                        for c in range(4):
                            at = (4 * s + c) * P
                            mm = pe.transpose(ps[:, c * P:(c + 1) * P], flat[:, at:at + P], ident[:])
                        give(mm, f"probsT{t}{s}")

                def attend_values(t):
                    ps = take(f"attn{t}")
                    was_read(f"probsT{t}0")
                    was_read(f"probsT{t}1")
                    pe.wait_ge(v_blocks_ready, 1)
                    w = 2 * (DK + 1)
                    for c in range(PAIRS):
                        mm = pe.matmul(ps[:, c * w:(c + 1) * w], probsT[:, t, c, :],
                                       v_blocks[:, c, :, :].rearrange("p a d -> p (a d)"), start=True, stop=True)
                    give(mm, f"attn{t}")

                def turn_attn():
                    ps = take("attnT")
                    for t in range(TILES):
                        mm = pe.transpose(ps[:, t * P:(t + 1) * P], attn[:, t, :], ident[:])
                    give(mm, "attnT")

                def project_out():
                    ps = take("proj")
                    was_read("attnT")
                    for t in range(TILES):
                        mm = pe.matmul(ps[:, t * D:(t + 1) * D], attnT[:, t, :], wT[:, 3, :], start=True, stop=True)
                    give(mm, "proj")

                def turn_norm():
                    ps = take("normT")
                    pe.wait_ge(xn_ready, 1)
                    for t in range(TILES):
                        mm = pe.transpose(ps[:, t * P:(t + 1) * P], xn[:, t, :], ident[:])
                    give(mm, "normT")

                def similarities(t):
                    ps = take(f"sims{t}")
                    was_read("normT")
                    give(pe.matmul(ps[:], xnT[:, t * P:(t + 1) * P], sim_w[:], start=True, stop=True), f"sims{t}")

                def turn_sims(t, s):
                    pe.wait_ge(sims_split[t], 1)
                    ps = take(f"simsT{t}{s}")
                    for k in range(4):
                        src = sims_hl[:, t, 4 * s + k, :, :].rearrange("p a b -> p (a b)").bitcast(F32)
                        mm = pe.transpose(ps[:, k * P:(k + 1) * P], src, ident[:])
                    give(mm, f"simsT{t}{s}")

                def was_kept(g):
                    if g % ITEMS in ACT_ITEMS:
                        pe.wait_ge(kept_by_act, count_items(ACT_ITEMS, first, g))
                    else:
                        pe.wait_ge(kept_by_dve, count_items(DVE_ITEMS, first, g))

                def pairs(g):
                    if user_before(g) >= first and (route or user_before(g) < 0):
                        was_kept(user_before(g))
                    if g % RH == 0:
                        t = g // RH % TILES
                        was_read(f"simsT{t}0")
                        was_read(f"simsT{t}1")
                    for s in range(2):
                        mm = pe.matmul(pair_ps[pair_buf(g)][:, s * HALF:(s + 1) * HALF],
                                       simsT[:, g // RH % TILES, g % RH, :], spread_r[:, s * HALF:(s + 1) * HALF],
                                       start=True, stop=False, skip_group_check=True)
                    mm.then_inc(pairs_ready, 1)

                def lower(g):
                    pe.wait_ge(below_ready, g + 1)
                    for s in range(2):
                        mm = pe.matmul(pair_ps[pair_buf(g)][:, s * HALF:(s + 1) * HALF], neg_ident[:],
                                       below[:, g % 2, s * HALF:(s + 1) * HALF],
                                       start=False, stop=True, skip_group_check=True)
                    mm.then_inc(lowered_for_act if g in ACT_ITEMS else lowered_for_dve, 1)

                def gather(t):
                    was_kept(-1 if t else RH - 1)
                    pe.wait_ge(kept_pooled, 1 if t else 1 + tail)
                    for s in range(2):
                        ps = take(f"kept{t}{s}")
                        for src in (kept_sum, kept_act):
                            for c in range(4):
                                mm = pe.matmul(ps[:, c * P:(c + 1) * P], src[:, t, s, c * P:(c + 1) * P], ident[:],
                                               is_transpose=True, start=(src is kept_sum and c == 0),
                                               stop=(src is kept_act), skip_group_check=True)
                        give(mm, f"kept{t}{s}")

                def mix(t):
                    ps = take(f"out{t}")
                    pe.wait_ge(gated, 1 if t else 1 + tail)
                    for c in range(CHUNKS):
                        mm = pe.matmul(ps[:, 0:D], gatedT[:, c, :], up_sb[:, c, :],
                                       start=(c == 0), stop=(c == CHUNKS - 1))
                    give(mm, f"out{t}")

                for g in range(ITEMS):
                    if route and g:
                        lower(g - 1)
                    wait_long = user_before(g + 1) >= g - 1
                    if (late if g == ITEMS - 1 else route) and not wait_long:
                        pairs(g + 1)
                    if route and g == 0:
                        turn_sims(1, 0)
                        turn_sims(1, 1)
                    if late and g == 1:
                        turn_attn()
                    if tail and g == 1:
                        gather(1)
                    if late and g == 2:
                        project_out()
                    if early and g == 2:
                        turn_inputs()
                    if early and g == 4:
                        project()
                    if route and g in (3, 4, 5):
                        for n in {3: (0,), 4: (1,), 5: (2, 3)}[g]:
                            if n == 0 and tail:
                                pe.wait_ge(gated, 1)
                            hidden(n)
                    if tail and g == 3:
                        mix(1)
                    if late and g == 6:
                        turn_norm()
                    if early and g == 6:
                        score(0)
                    if late and g == 7:
                        similarities(0)
                        similarities(1)
                    if early and g == 8:
                        score(1)
                    if route and g == 9:
                        gather(0)
                    if early and g in (10, 12):
                        turn_probs((g - 10) // 2)
                    if late and g in (11, 13):
                        turn_sims(0, (g - 11) // 2)
                    if route and g == 13:
                        mix(0)
                    if early and g in (12, 14):
                        attend_values((g - 12) // 2)
                    if begin:
                        setup_step(g)
                    if route and wait_long:
                        pairs(g + 1)
                    if route and g == 5:
                        pe.sem_inc(sims_split[1], -1)
                    if early and g == 2:
                        pe.sem_inc(ctx_loaded, -32)
                        pe.sem_inc(y_ready, -1)
                    if late and g == 6:
                        pe.sem_inc(xn_ready, -1)
                    if early and g == 8:
                        pe.sem_inc(k_blocks_ready, -1)
                    if (tail or route) and g == 9:
                        pe.sem_inc(kept_pooled, -(tail + route))
                    if early and g == 12:
                        pe.sem_inc(shifted, -TILES)
                    if late and g == 13:
                        pe.sem_inc(sims_split[0], -1)
                    if (tail or route) and g == 13:
                        pe.sem_inc(gated, -(tail + route))
                    if early and g == 14:
                        pe.sem_inc(v_blocks_ready, -1)

                if tail or route:
                    for kept, kind in ((kept_by_act, ACT_ITEMS), (kept_by_dve, DVE_ITEMS)):
                        n = count_items(kind, first, ITEMS - 3 if route else -1)
                        pe.wait_ge(kept, n)
                        pe.sem_inc(kept, -n)
                if route:
                    lower(ITEMS - 1)
                    pe.sem_inc(below_ready, -ITEMS)
                for b in range(2):
                    if used[b]:
                        pe.wait_ge(misc_read[b], used[b])
                        pe.sem_inc(misc_read[b], -used[b])

            iteration(False, False, False, True, begin=True)
            iteration(False, False, True, True)
            iteration(False, True, True, True)
            iteration(True, True, True, True)
            with pe.Fori(0, (BATCH - 4) // 2):
                iteration(True, True, True, True)
                iteration(True, True, True, True)
            iteration(True, True, True, False)
            iteration(True, True, False, False)
            iteration(True, False, False, False)

        @block.scalar
        def _(act):
            act.wait_ge(attention_loaded, 16 * 7)
            nc.scalar.activation(neg_ident[:], ident[:], ACT.Identity, scale=-1.0)
            nc.scalar.activation(bk_scaled[:], bk[:], ACT.Identity, scale=float(DK) ** -0.5)

            def copy_weights(n, done, dst):
                act.wait_ge(setup_pe, done)
                nc.scalar.activation(dst, banks[n].rearrange("p (a b) -> p a b", a=4), ACT.Copy).then_inc(setup_act, 1)

            def copy_down(n, done, dst):
                act.wait_ge(setup_pe, done)
                nc.scalar.activation(dst, banks[n].rearrange("p (a b) -> p a b", a=4), ACT.Copy,
                                     scale=nw[:, 0:1]).then_inc(setup_act, 1)

            def setup_step(g):
                if g == 6:
                    copy_weights(0, 2, wqT[:, 0:4, :])
                    copy_weights(1, 3, wqT[:, 4:8, :])
                if g == 8:
                    copy_weights(2, 4, wqT[:, 8:12, :])
                    copy_weights(3, 5, wqT[:, 12:16, :])
                    copy_weights(4, 6, keysT[:].rearrange("p g s k -> p (g s) k"))
                if g == 9:
                    copy_down(5, 7, downT[:, 0:4, :])
                if g == 11:
                    copy_down(1, 8, downT[:, 4:8, :])
                if g == 13:
                    act.wait_ge(setup_pe, 9)
                    nc.scalar.activation(sim_w[:], banks[0], ACT.Copy, scale=nw[:, 0:1])
                    act.wait_ge(others_loaded, 16 * 2)
                    nc.scalar.activation(spread_r[:], spread_f[:], ACT.Identity).then_inc(setup_act, 1)

            copy_weights(6, 1, wT[:])

            def iteration(tail, route, late, early, begin=False):
                plan, _, read = misc_plan(tail, route, late, early)

                def take(name):
                    b, _, k, _ = plan[name]
                    act.wait_ge(misc_for[b, "act"], k + 1)
                    return misc_ps[b], misc_read[b]

                def find_below(g):
                    act.wait_ge(pairs_ready, g + 1)
                    nc.scalar.activation(below[:, g % 2, :], pair_ps[pair_buf(g)][:], ACT.Relu, scale=-STEEP,
                                         bias=steep_cut[:, g // RH, g % RH:g % RH + 1]).then_inc(below_ready, 1)

                def keep(g):
                    t = g // RH
                    n = TILE_ACT_ITEMS[t].index(g)
                    dst = kept_act[:, t] if n == 0 else kept_a[:, n - 1]
                    act.wait_ge(lowered_for_act, count_items(ACT_ITEMS, 0, g))
                    nc.scalar.activation(dst.rearrange("p s e -> p (s e)"), pair_ps[pair_buf(g)][:],
                                         ACT.Relu).then_inc(kept_by_act, 1)
                    if n:
                        nc.scalar.copy(flag[:, 5 + n:6 + n], ident[:, 0:1]).then_inc(kept_for_pool, 1)

                def turn_sims(t, s):
                    ps, done = take(f"simsT{t}{s}")
                    nc.scalar.activation(simsT[:, t, 4 * s:4 * s + 4, :],
                                         ps[:].rearrange("p (a b) -> p a b", a=4), ACT.Identity).then_inc(done, 1)

                def exps(t):
                    for s in range(2):
                        ps, done = take(f"probsT{t}{s}")
                        nc.scalar.activation(probsT[:, t, 4 * s:4 * s + 4, :],
                                             ps[:].rearrange("p (a b) -> p a b", a=4), ACT.Exp).then_inc(done, 1)

                def copy_high(t, src):
                    return nc.scalar.activation(sims_hl[:, t, :, 0, :], src, ACT.Identity)

                def copy_sims(t):
                    ps, done = take(f"sims{t}")
                    ins = nc.scalar.activation(sims[:, t, :, :, :].rearrange("p h s k -> p (h s k)"), ps[:],
                                               ACT.Identity)
                    if t == 0:
                        ins.then_inc(sims_for_topk[0], 1)
                        copy_high(0, ps[:].rearrange("p (h k) -> p h k", h=RH)).then_inc(done, 1)
                        nc.scalar.copy(flag[:, 3:4], ident[:, 0:1]).then_inc(sims_to_split, 1)
                    else:
                        ins.then_inc(done, 1)
                        nc.scalar.copy(flag[:, 8:9], ident[:, 0:1]).then_inc(sims_for_topk[1], 1)
                        nc.scalar.copy(flag[:, 9:10], ident[:, 0:1]).then_inc(act_step, 1)

                def copy_scores(t):
                    for s in range(2):
                        ps, done = take(f"scores{t}{s}")
                        nc.scalar.activation(
                            scores[:, t, 8 * s:8 * s + 8, :], ps[:].rearrange("p (h k) -> p h k", h=8),
                            ACT.Identity).then_inc(done, 1)
                    nc.scalar.copy(flag[:, 1 + t:2 + t], ident[:, 0:1]).then_inc(scores_ready, 1)

                def load_table(func):
                    nc.scalar.activation(flag[:, 0:1], ident[:, 0:1], func)

                def gelu(n):
                    ps, done = take(f"hidden{n}")
                    nc.scalar.activation(geluT[:, 2 * n:2 * n + 2, :], ps[:].rearrange("p (a b) -> p a b", a=2),
                                         ACT.Gelu).then_inc(done, 1)

                for g in range(ITEMS):
                    if route and g % RH == 0:
                        act.wait_ge(cut_ready[g // RH], 1)
                    if route:
                        find_below(g)
                        if g % RH == 0:
                            act.sem_inc(cut_ready[g // RH], -1)
                    if late and g == 6:
                        ps, done = take("normT")
                        nc.scalar.activation(xnT[:], ps[:, 0:SEQ], ACT.Identity).then_inc(done, 1)
                    if route and g - 1 in ACT_ITEMS:
                        keep(g - 1)
                    if route and g == 0:
                        turn_sims(1, 0)
                        turn_sims(1, 1)
                    if late and g == 1:
                        ps, done = take("attnT")
                        nc.scalar.activation(attnT[:].rearrange("p t q -> p (t q)"), ps[:, 0:TILES * P],
                                             ACT.Identity).then_inc(done, 1)
                    if route and g == 1:
                        load_table(ACT.Gelu)
                    if early and g == 2:
                        ps, done = take("inputsT")
                        nc.scalar.activation(ctxT[:], ps[:, 0:P], ACT.Identity)
                        nc.scalar.activation(yT[:], ps[:, P:P + SEQ], ACT.Identity).then_inc(done, 1)
                    if early and g == 4:
                        ps, done = take("qkv")
                        nc.scalar.activation(kT[:], ps[:, SEQ:SEQ + CTX], ACT.Identity,
                                             scale=float(DK) ** -0.5, bias=bk_scaled[:, 0:1])
                        nc.scalar.activation(v_in[:], ps[:, SEQ + CTX:SEQ + CTX + D], ACT.Identity).then_inc(v_ready, 1)
                        nc.scalar.activation(qT[:], ps[:, 0:SEQ], ACT.Identity, bias=bq[:, 0:1]).then_inc(done, 1)
                    if route and g in (3, 4, 5):
                        for n in {3: (0,), 4: (1,), 5: (2, 3)}[g]:
                            gelu(n)
                    if route and g == 5:
                        nc.scalar.copy(flag[:, 5:6], ident[:, 0:1]).then_inc(gelu_ready, 1)
                    if early and g == 6:
                        copy_scores(0)
                    if late and g in (7, 8):
                        copy_sims(g - 7)
                    if early and g == 8:
                        copy_scores(1)
                    if late and g == 14:
                        act.wait_ge(act_step, 1)
                        act.sem_inc(act_step, -1)
                        copy_high(1, sims[:, 1].rearrange("p h s k -> p h (s k)")).then_inc(sims_to_split, 1)
                    if early and g == 9:
                        load_table(ACT.Exp)
                    if early and g in (10, 12):
                        exps((g - 10) // 2)
                    if late and g in (11, 13):
                        turn_sims(0, (g - 11) // 2)
                    if begin:
                        setup_step(g)

                if route:
                    act.sem_inc(pairs_ready, -ITEMS)
                    act.sem_inc(lowered_for_act, -len(ACT_ITEMS))
                for b in range(2):
                    if read.get((b, "act")):
                        act.sem_inc(misc_for[b, "act"], -read[b, "act"])

            iteration(False, False, False, True, begin=True)
            iteration(False, False, True, True)
            iteration(False, True, True, True)
            iteration(True, True, True, True)
            with act.Fori(0, (BATCH - 4) // 2):
                iteration(True, True, True, True)
                iteration(True, True, True, True)
            iteration(True, True, True, False)
            iteration(True, True, False, False)
            iteration(True, False, False, False)

        @block.gpsimd
        def _(pool):
            nc.gpsimd.memset(neg_half[:], -0.5)
            pool.drain()

            def setup():
                pool.wait_ge(blocks_loaded, 16 * 4)
                nc.gpsimd.tensor_copy(v_blocks[:, :, :, DK],
                                      pair_mask[:].unsqueeze(1).to_broadcast([P, PAIRS, 2]))

            def iteration(tail, route, late, early, begin=False):
                steps = [0]

                def inverse_root(dst, tmp, var, scale, shift):
                    nc.gpsimd.tensor_scalar(tmp[:], var, scale, shift, ALU.mult, ALU.add).then_inc(pool_step, 1)
                    steps[0] += 1
                    pool.wait_ge(pool_step, steps[0])
                    nc.gpsimd.tensor_tensor(dst[:], tmp[:], neg_half[:], ALU.pow).then_inc(rstd_ready, 1)

                def pair_cands(t, q):
                    pool.wait_ge(halves_sorted, (q + 1 if t else q + 1 + 2 * route))
                    hs = slice(4 * q, 4 * q + 4)
                    at = 0
                    for i0, ni, nj in RECTS:
                        a = sorted16[:, t, hs, 0, i0:i0 + ni].unsqueeze(3).to_broadcast([P, 4, ni, nj])
                        b = sorted16[:, t, hs, 1, 0:nj].unsqueeze(2).to_broadcast([P, 4, ni, nj])
                        dst = cands[:, t, hs, at:at + ni * nj].rearrange("p h (i j) -> p h i j", i=ni)
                        last = nc.gpsimd.tensor_tensor(dst, a, b, ALU.add)
                        at += ni * nj
                    last.then_inc(cands_ready, 1)

                def blocks():
                    pool.wait_ge(v_ready, 1)
                    shape = [P, HEADS, CTX]
                    nc.gpsimd.tensor_tensor(k_blocks[:], kT[:].unsqueeze(1).to_broadcast(shape),
                                            mask[:].unsqueeze(2).to_broadcast(shape), ALU.mult).then_inc(k_blocks_ready, 1)
                    nc.gpsimd.tensor_tensor(v_biased[:], v_in[:], bv[:], ALU.add).then_inc(pool_step, 1)
                    steps[0] += 1
                    pool.wait_ge(pool_step, steps[0])
                    nc.gpsimd.tensor_tensor(v_blocks[:, :, :, 0:DK],
                                            v_biased[:].rearrange("p (c a d) -> p c a d", a=2, d=DK),
                                            pair_mask[:].unsqueeze(1).unsqueeze(3).to_broadcast([P, PAIRS, 2, DK]),
                                            ALU.mult).then_inc(v_blocks_ready, 1)
                    nc.gpsimd.memset(pool_mark[:], 0.0).then_inc(inputs_read, 1)

                def shift_scores(t):
                    pool.wait_ge(peak_ready, t + 1)
                    nc.gpsimd.tensor_tensor(scores[:, t], scores[:, t],
                                            peak[:, t, :].unsqueeze(2).to_broadcast([P, HEADS, CTX]),
                                            ALU.subtract).then_inc(shifted, 1)

                def split(t):
                    pool.wait_ge(sims_to_split, t + 1)
                    nc.gpsimd.tensor_tensor(
                        sims_hl[:, t, :, 1, :], sims[:, t, :, :, :].rearrange("p h s k -> p h (s k)"),
                        sims_hl[:, t, :, 0, :].bitcast(F32), ALU.subtract).then_inc(sims_split[t], 1)

                def add_act(t, n):
                    pool.wait_ge(kept_for_pool, 2 * t + n + 1)
                    if n == 1:
                        pool.wait_ge(pool_step, added[t])
                    ins = nc.gpsimd.tensor_tensor(kept_act[:, t], kept_act[:, t], kept_a[:, n], ALU.add)
                    if n == 0:
                        ins.then_inc(pool_step, 1)
                        steps[0] += 1
                        added[t] = steps[0]
                    else:
                        ins.then_inc(kept_pooled, 1)

                added = {}
                if early:
                    pool.wait_ge(var_ready, 1)
                    inverse_root(rstd, shifted_var, mean_var[:, :, 1], 1.0, EPS)
                if begin:
                    setup()
                if late:
                    pool.wait_ge(var_ready, 1 + early)
                    inverse_root(rstd2, shifted_var2, mean_var2[:, :, 1], 1.0 + EPS, EPS * EPS)
                if early:
                    for t in range(TILES):
                        nc.gpsimd.tensor_tensor(x_bias[:, t, :], x_in[:, t, :], bo[:], ALU.add)
                if route:
                    pair_cands(1, 0)
                    add_act(0, 0)
                if early:
                    blocks()
                if route:
                    pair_cands(1, 1)
                    add_act(0, 1)
                if early:
                    shift_scores(0)
                if late:
                    split(0)
                if early:
                    shift_scores(1)
                if late:
                    pair_cands(0, 0)
                    pair_cands(0, 1)
                if route:
                    add_act(1, 0)
                if late:
                    split(1)
                if route:
                    add_act(1, 1)

                if early:
                    pool.sem_inc(v_ready, -1)
                    pool.sem_inc(peak_ready, -TILES)
                if late:
                    pool.sem_inc(sims_to_split, -TILES)
                if late or early:
                    pool.sem_inc(var_ready, -(late + early))
                if steps[0]:
                    pool.wait_ge(pool_step, steps[0])
                    pool.sem_inc(pool_step, -steps[0])
                if route:
                    pool.sem_inc(kept_for_pool, -2 * TILES)
                if route or late:
                    pool.sem_inc(halves_sorted, -2 * (route + late))

            iteration(False, False, False, True, begin=True)
            iteration(False, False, True, True)
            iteration(False, True, True, True)
            iteration(True, True, True, True)
            with pool.Fori(0, (BATCH - 4) // 2):
                iteration(True, True, True, True)
                iteration(True, True, True, True)
            iteration(True, True, True, False)
            iteration(True, True, False, False)
            iteration(True, False, False, False)

        @block.vector
        def _(dve):
            def iteration(tail, route, late, early):
                plan, _, read = misc_plan(tail, route, late, early)
                steps = [0]

                def step(ins):
                    ins.then_inc(dve_step, 1)
                    steps[0] += 1
                    return steps[0]

                def take(name):
                    b, _, k, _ = plan[name]
                    dve.wait_ge(misc_for[b, "dve"], k + 1)
                    return misc_ps[b], misc_read[b]

                def variance(src, st, mv):
                    for t in range(TILES):
                        n = step(nc.vector.bn_stats(st[:, t, :], src[:, t, :]))
                    dve.wait_ge(dve_step, n)
                    nc.vector.bn_aggr(mv[:, 0, :], st[:, 0, :])
                    nc.vector.bn_aggr(mv[:, 1, :], st[:, 1, :]).then_inc(var_ready, 1)

                def normalise(dst, src, mv, r, ready):
                    for t in range(TILES):
                        last = nc.vector.tensor_scalar(dst[:, t, :], src[:, t, :], mv[:, t, 0:1], r[:, t:t + 1],
                                                       ALU.subtract, ALU.mult)
                    last.then_inc(ready, 1)

                reached = {}
                summed = [0]

                def lists(q):
                    return [(h, s) for h in range(4 * q, 4 * q + 4) for s in range(2)]

                def sort_first(t, q):
                    for h, s in lists(q):
                        reached[t, h, s] = step(nc.vector.max(sorted16[:, t, h, s, 0:8], sims[:, t, h, s, :]))

                def sort_rest(t, q):
                    for h, s in lists(q):
                        dve.wait_ge(dve_step, reached[t, h, s])
                        reached[t, h, s] = step(nc.vector.match_replace(
                            rest[:, t, h, s, :], sorted16[:, t, h, s, 0:8], sims[:, t, h, s, :], LOWEST))

                def sort_second(t, q):
                    for h, s in lists(q):
                        dve.wait_ge(dve_step, reached[t, h, s])
                        last = nc.vector.max(sorted16[:, t, h, s, 8:16], rest[:, t, h, s, :])
                    last.then_inc(halves_sorted, 1)

                def best_first(t, q):
                    dve.wait_ge(cands_ready, q + 1 if t else q + 1 + 2 * route)
                    for h in range(4 * q, 4 * q + 4):
                        reached[t, h] = step(nc.vector.max(best[:, t, h, 0:8], cands[:, t, h, :]))

                def best_rest(t, q):
                    for h in range(4 * q, 4 * q + 4):
                        dve.wait_ge(dve_step, reached[t, h])
                        reached[t, h] = step(nc.vector.match_replace(
                            cands_rest[:, t, h, :], best[:, t, h, 0:8], cands[:, t, h, :], LOWEST))

                def best_second(t, q):
                    for h in range(4 * q, 4 * q + 4):
                        dve.wait_ge(dve_step, reached[t, h])
                        reached[t, h] = step(nc.vector.max(best[:, t, h, 8:16], cands_rest[:, t, h, :]))

                def set_cut(t):
                    m = step(nc.vector.tensor_tensor(top_sim[:, t, :], sorted16[:, t, :, 0, 0], sorted16[:, t, :, 1, 0],
                                                     ALU.max))
                    dve.wait_ge(dve_step, max(m, reached[t, RH - 1]))
                    n = step(nc.vector.scalar_tensor_tensor(cut_raw[:, t, :], top_sim[:, t, :], -MARGIN,
                                                            best[:, t, :, TOP - 1], ALU.mult, ALU.add))
                    dve.wait_ge(dve_step, n)
                    n = step(nc.vector.tensor_scalar(cut[:, t, :], cut_raw[:, t, :], TINY, None, ALU.max))
                    dve.wait_ge(dve_step, n)
                    nc.vector.tensor_scalar(steep_cut[:, t, :], cut[:, t, :], STEEP, None, ALU.mult)\
                        .then_inc(cut_ready[t], 1)

                def find_peak(t):
                    dve.wait_ge(scores_ready, t + 1)
                    nc.vector.tensor_reduce(peak[:, t, :], scores[:, t], AX.X, ALU.max).then_inc(peak_ready, 1)

                search = (
                    {8: [(sort_first, 0), (sort_rest, 0)], 10: [(sort_second, 0)], 11: [(sort_first, 1)],
                     12: [(sort_rest, 1), (sort_second, 1), (best_first, 0)],
                     13: [(best_rest, 0), (best_second, 0), (best_first, 1)],
                     14: [(best_rest, 1)], 15: [(best_second, 1)]},
                    {0: [(sort_first, 0)], 2: [(sort_rest, 0)], 3: [(sort_second, 0), (sort_first, 1)],
                     4: [(sort_rest, 1)], 5: [(sort_second, 1), (best_first, 0)],
                     6: [(best_rest, 0), (best_second, 0), (best_first, 1), (best_rest, 1), (best_second, 1)]},
                )
                if not route:
                    search = ({8: [(sort_first, 0), (sort_rest, 0), (sort_second, 0),
                                   (sort_first, 1), (sort_rest, 1), (sort_second, 1)],
                               10: [(best_first, 0), (best_rest, 0), (best_second, 0),
                                    (best_first, 1), (best_rest, 1), (best_second, 1)]}, {})

                def threshold(t, g):
                    for step_of_search, q in search[t].get(g, []):
                        step_of_search(t, q)
                    if g == max(search[t]):
                        set_cut(t)

                def add_kept(g):
                    t = g // RH
                    dve.wait_ge(lowered_for_dve, count_items(DVE_ITEMS, 0, g))
                    after = g - 1 in DVE_ITEMS and (g - 1) // RH == t
                    if after:
                        dve.wait_ge(dve_step, summed[0])
                    total = kept_sum[:, t].rearrange("p s e -> p (s e)")
                    ps = pair_ps[pair_buf(g)][:]
                    if count_items(DVE_ITEMS, t * RH, g) == 1:
                        ins = nc.vector.tensor_scalar(total, ps, 0.0, None, ALU.max)
                    else:
                        ins = nc.vector.scalar_tensor_tensor(total, ps, 0.0, total, ALU.max, ALU.add)
                    ins.then_inc(kept_by_dve, 1)
                    if g + 1 in DVE_ITEMS and (g + 1) // RH == t:
                        summed[0] = step(nc.vector.memset(mark[:, 2:3], 0.0))

                def divide(t):
                    ps, done = take(f"attn{t}")
                    v = ps[:, 0:HEADS * (DK + 1)].rearrange("p (h d) -> p h d", d=DK + 1)
                    n = step(nc.vector.reciprocal(rsum[:, t, :], v[:, :, DK]))
                    dve.wait_ge(dve_step, n)
                    nc.vector.tensor_tensor(attn[:, t, :].rearrange("p (h d) -> p h d", d=DK), v[:, :, 0:DK],
                                            rsum[:, t, :].unsqueeze(2).to_broadcast([P, HEADS, DK]),
                                            ALU.mult).then_inc(done, 1)

                def residual():
                    ps, done = take("proj")
                    n = step(nc.vector.tensor_tensor(x1_new[:, 0, :], ps[:, 0:D], x_bias[:, 0, :], ALU.add))
                    nc.vector.tensor_tensor(x1_new[:, 1, :], ps[:, D:2 * D], x_bias[:, 1, :], ALU.add).then_inc(done, 1)
                    dve.wait_ge(dve_step, n)
                    n = step(nc.vector.bn_stats(stats2[:, 0, :], x1_new[:, 0, :]))
                    dve.wait_ge(dve_step, n)
                    n = step(nc.vector.bn_stats(stats2[:, 1, :], x1_new[:, 1, :]))
                    dve.wait_ge(dve_step, n)
                    nc.vector.bn_aggr(mean_var2[:, 0, :], stats2[:, 0, :])
                    nc.vector.bn_aggr(mean_var2[:, 1, :], stats2[:, 1, :]).then_inc(var_ready, 1)

                def gate(t):
                    if t == 0:
                        dve.wait_ge(gelu_ready, 1)
                    for s in range(2):
                        ps, done = take(f"kept{t}{s}")
                        nc.vector.tensor_tensor(gatedT[:, 4 * s:4 * s + 4, :], ps[:].rearrange("p (c t) -> p c t", c=4),
                                                geluT[:, 4 * s:4 * s + 4, t * P:(t + 1) * P], ALU.mult)\
                            .then_inc(done, 1)
                    nc.vector.memset(mark[:, 3:4], 0.0).then_inc(gated, 1)

                def finish(t):
                    if t == 0 and tail:
                        dve.wait_ge(out_free, 1)
                    ps, done = take(f"out{t}")
                    nc.vector.tensor_tensor(y_out[:, t, :], ps[:, 0:D], x1_tail[:] if t else x1[:, 0, :],
                                            ALU.add).then_inc(done, 1)
                    nc.vector.memset(mark[:, t:t + 1], 0.0).then_inc(out_ready, 1)

                for g in range(ITEMS):
                    if route and g - 1 in DVE_ITEMS:
                        add_kept(g - 1)
                    if route and g == 14:
                        finish(0)
                    if early and g == 0:
                        dve.wait_ge(x_loaded, 16)
                        variance(x_in, stats, mean_var)
                    if tail and g == 0:
                        n = step(nc.vector.tensor_copy(x1_tail[:], x1[:, 1, :]))
                        dve.wait_ge(dve_step, n)
                    if route and g == 0:
                        nc.vector.tensor_copy(x1[:], x1_new[:])
                    if tail and g == 1:
                        gate(1)
                    if late and g == 2:
                        residual()
                    if early and g == 1:
                        dve.wait_ge(rstd_ready, 1)
                        normalise(y, x_in, mean_var, rstd, y_ready)
                    if route and g < RH:
                        if g == 0:
                            dve.wait_ge(sims_for_topk[1], 1)
                        threshold(1, g)
                        if g == 0:
                            dve.sem_inc(sims_for_topk[1], -1)
                    if early and g in (13, 15):
                        divide((g - 13) // 2)
                    if late and g >= RH:
                        if g == RH:
                            dve.wait_ge(sims_for_topk[0], 1)
                        threshold(0, g)
                        if g == RH:
                            dve.sem_inc(sims_for_topk[0], -1)
                    if route and g == 9:
                        gate(0)
                        dve.sem_inc(gelu_ready, -1)
                    if early and g == 9:
                        find_peak(1)
                        dve.sem_inc(scores_ready, -TILES)
                    if late and g == 4:
                        dve.wait_ge(rstd_ready, 1 + early)
                        normalise(xn, x1_new, mean_var2, rstd2, xn_ready)
                    if tail and g == 3:
                        finish(1)
                    if early and g == 7:
                        find_peak(0)
                    if early and g == 0:
                        dve.sem_inc(x_loaded, -16)
                    if (late or early) and g == 4:
                        dve.sem_inc(rstd_ready, -(late + early))
                    if (route or late) and g == 15:
                        dve.sem_inc(cands_ready, -2 * (route + late))
                    if tail and route and g == 14:
                        dve.sem_inc(out_free, -1)

                if route:
                    add_kept(ITEMS - 1)
                    dve.sem_inc(lowered_for_dve, -len(DVE_ITEMS))
                for b in range(2):
                    if read.get((b, "dve")):
                        dve.sem_inc(misc_for[b, "dve"], -read[b, "dve"])
                if steps[0]:
                    dve.wait_ge(dve_step, steps[0])
                    dve.sem_inc(dve_step, -steps[0])

            iteration(False, False, False, True)
            iteration(False, False, True, True)
            iteration(False, True, True, True)
            iteration(True, True, True, True)
            with dve.Fori(0, (BATCH - 4) // 2):
                iteration(True, True, True, True)
                iteration(True, True, True, True)
            iteration(True, True, True, False)
            iteration(True, True, False, False)
            iteration(True, False, False, False)


_INS = [("x", "x"), ("ctx_1024", "ctx"), ("L0_xattn_W_Q", "W_Q"), ("L0_xattn_b_Q", "b_Q"), ("L0_xattn_W_K", "W_K"),
        ("L0_xattn_b_K", "b_K"), ("L0_xattn_W_V", "W_V"), ("L0_xattn_b_V", "b_V"), ("L0_xattn_W_O", "W_O"),
        ("L0_xattn_b_O", "b_O"), ("L0_ffn_norm_w", "norm_w"), ("L0_ffn_wq", "wq"), ("L0_ffn_keys", "keys"),
        ("L0_ffn_expert_down", "down"), ("L0_ffn_expert_up", "up")]


def kernel(**inputs):
    import numpy as np
    import concourse.bacc as bacc
    from concourse import mybir as mb
    from concourse.bass_utils import run_bass_kernel_spmd

    arrays = {f"in_{short}": np.ascontiguousarray(inputs[name]) for name, short in _INS}
    arrays["in_eye"] = np.eye(P, dtype=np.float32)
    row, col = np.arange(P)[:, None] % (2 * NK), np.arange(EXPERTS)[None, :]
    arrays["in_spread"] = ((row == col // NK) | (row == NK + col % NK)).astype(np.float32)
    arrays["in_head_mask"] = (np.arange(P)[:, None] // DK == np.arange(HEADS)[None, :]).astype(np.float32)
    arrays["in_key_mask"] = (np.arange(P)[:, None] // CTX == np.arange(2)[None, :]).astype(np.float32)

    nc = bacc.Bacc("TRN2", target_bir_lowering=False, num_devices=1)
    aps = [nc.dram_tensor(n, a.shape, mb.dt.from_np(a.dtype), kind="ExternalInput").ap() for n, a in arrays.items()]
    out = nc.dram_tensor("out", (BATCH, SEQ, D), mb.dt.float32, kind="ExternalOutput").ap()
    xattn_peer_kernel(nc, *aps, out)
    r = run_bass_kernel_spmd(nc, [arrays], core_ids=[0])
    return r.results[0]["out"]
```
